# Optimizing a Trainium2 kernel written in Bass

```python
import numpy as np
import jax
import jax.numpy as jnp

def _softmax(x, axis=-1):
    return jax.nn.softmax(x, axis=axis)

def _gelu(x):
    return jax.nn.gelu(x, approximate=True)

def _silu(x):
    return jax.nn.silu(x)

def _sigmoid(x):
    return jax.nn.sigmoid(x)

def _layernorm(x, axis=-1, eps=1e-05):
    m = jnp.mean(x, axis=axis, keepdims=True)
    v = jnp.var(x, axis=axis, keepdims=True)
    return (x - m) / jnp.sqrt(v + eps)

def _scatter_add(tgt, idx, src, axis=0):
    return tgt.at[idx].add(src)

def _segment_sum(src, seg, n):
    return jax.ops.segment_sum(src, seg, n)
kernel_name = 'mk_xattn_ffn_d1_seqx_r2_7ef802'

def setup_inputs(seed: int=0):
    np.random.seed(seed)
    _w = jnp.asarray

    def _rec_inputs():
        import jax
        import jax.numpy as jnp
        _rk = jax.random.key(seed)
        x = -0.0003929 + 0.9999 * jax.random.normal(jax.random.fold_in(_rk, 1), (16, 256, 2048), jnp.float32)
        _lenS = 256 - jax.random.randint(jax.random.fold_in(_rk, 7), (16,), 0, max(1, 256 // 4) + 1, jnp.int32)
        _lenS2 = 256 - jax.random.randint(jax.random.fold_in(_rk, 8), (16,), 0, max(1, 256 // 4) + 1, jnp.int32)
        _ctx_1024P = jax.random.normal(jax.random.fold_in(_rk, 11), (16, 16, 512), jnp.float32)
        _ctx_1024c = jax.random.dirichlet(jax.random.fold_in(_rk, 511), 0.3 * jnp.ones((16,), jnp.float32), (16, 256))
        _ctx_1024t = jnp.einsum('bsk,bkd->bsd', _ctx_1024c, _ctx_1024P)
        _ctx_1024t = _ctx_1024t * jax.lax.rsqrt(jnp.mean(jnp.square(_ctx_1024t)) + 1e-12) * 0.953939
        ctx_1024 = -1.39393e-06 + 0.999914 * (_ctx_1024t + 0.3 * jax.random.normal(jax.random.fold_in(_rk, 611), (16, 256, 512), jnp.float32))
        _validS = jnp.arange(256)[None, :] < _lenS[:, None]
        _validS2 = jnp.arange(256)[None, :] < _lenS2[:, None]
        _causal = jnp.tril(jnp.ones((256, 256), dtype=bool))
        mask_SxS2_ff0 = jnp.where(jnp.ones((256, 256), dtype=bool), 0.0, -1000000000.0).astype(jnp.float32)
        return (x, ctx_1024, mask_SxS2_ff0)
    x, ctx_1024, mask_SxS2_ff0 = _rec_inputs()

    def _L0_xattn_setup():
        import math
        import jax, jax.numpy as jnp
        import numpy as np
        N_HEADS = 32
        N_KV_HEADS = 8
        N_REP = N_HEADS // N_KV_HEADS
        HEAD_DIM = 2048 // N_HEADS
        key = jax.random.key(seed)
        kq, kk, kv = jax.random.split(key, 3)
        B, S, T = (2, 1024, 1024)
        q = jax.random.normal(kq, (B, S, N_HEADS * HEAD_DIM), dtype=jnp.float32)
        k = jax.random.normal(kk, (B, T, N_KV_HEADS * HEAD_DIM), dtype=jnp.float32)
        v = jax.random.normal(kv, (B, T, N_KV_HEADS * HEAD_DIM), dtype=jnp.float32)
        mask = jnp.zeros((S, T), dtype=jnp.float32)
        return {'q': q, 'k': k, 'v': v, 'start_pos': 0, 'mask': mask}
    _L0_xattn_all = _L0_xattn_setup()
    _L0_xattn_in = {k: v for k, v in _L0_xattn_all.items() if k in ()}
    del _L0_xattn_all

    def _L0_ffn_setup():
        import jax, jax.numpy as jnp
        import numpy as np
        ALPHA = 32
        R = 16
        SCALING = ALPHA / R
        key = jax.random.key(seed)
        k1, k2, k3, k4 = jax.random.split(key, 4)
        B_, S, D = (4, 1024, 2048)
        H, r, O = (8, R, 2048)
        x = jax.random.normal(k1, (B_, S, D), dtype=jnp.float32)
        A = jax.random.normal(k2, (H, r, D), dtype=jnp.float32) * 0.02
        Bm = jax.random.normal(k3, (H, O, r), dtype=jnp.float32) * 0.02
        Wr = jax.random.normal(k4, (H, D), dtype=jnp.float32) * 0.02
        br = jnp.zeros((H,), dtype=jnp.float32)
        return {'x': x, 'A': A, 'B': Bm, 'Wr': Wr, 'br': br}
    _L0_ffn_all = _L0_ffn_setup()
    _L0_ffn_in = {k: v for k, v in _L0_ffn_all.items() if k in ('A', 'B', 'Wr', 'br')}
    del _L0_ffn_all
    return {'x': x, 'ctx_1024': ctx_1024, 'mask_SxS2_ff0': mask_SxS2_ff0, 'L0_ffn_A': _L0_ffn_in['A'], 'L0_ffn_B': _L0_ffn_in['B'], 'L0_ffn_Wr': _L0_ffn_in['Wr'], 'L0_ffn_br': _L0_ffn_in['br']}

def reference(x, ctx_1024, mask_SxS2_ff0, L0_ffn_A, L0_ffn_B, L0_ffn_Wr, L0_ffn_br):
    import jax
    import jax.numpy as jnp

    def _L0_xattn_ref(q, k, v, start_pos, mask):
        import math
        import jax, jax.numpy as jnp
        import numpy as np
        N_HEADS = 32
        N_KV_HEADS = 8
        N_REP = N_HEADS // N_KV_HEADS
        HEAD_DIM = 2048 // N_HEADS
        b, s, _ = q.shape
        t = k.shape[1]
        xq = q.reshape(b, s, N_KV_HEADS, N_REP, HEAD_DIM)
        xk = k.reshape(b, t, N_KV_HEADS, HEAD_DIM)
        xv = v.reshape(b, t, N_KV_HEADS, HEAD_DIM)
        scores = jnp.einsum('bsgrd,btgd->bgrst', xq, xk) / math.sqrt(HEAD_DIM)
        scores = scores + mask
        probs = jax.nn.softmax(scores.astype(jnp.float32), axis=-1).astype(q.dtype)
        out = jnp.einsum('bgrst,btgd->bsgrd', probs, xv)
        return out.reshape(b, s, N_HEADS * HEAD_DIM)

    def _L0_ffn_ref(x, A, B, Wr, br):
        import jax, jax.numpy as jnp
        import numpy as np
        ALPHA = 32
        R = 16
        SCALING = ALPHA / R
        H = A.shape[0]
        router_logits = jnp.einsum('bsd,hd->bsh', x, Wr) + br
        scores = H * jax.nn.softmax(router_logits, axis=-1)
        low = jnp.einsum('bsd,hrd->bshr', x, A)
        out = jnp.einsum('bshr,hor,bsh->bso', low, B, scores)
        return SCALING * out
    x = x + _L0_xattn_ref(_layernorm(x, axis=-1), ctx_1024, ctx_1024, 0, mask_SxS2_ff0)
    x = x + _L0_ffn_ref(_layernorm(x, axis=-1), L0_ffn_A, L0_ffn_B, L0_ffn_Wr, L0_ffn_br)
    return x

_drawn_inputs = setup_inputs


def setup_inputs(seed=0):
    import zlib

    import numpy as np

    out = dict(_drawn_inputs(seed))
    spreads = {'mask_SxS2_ff0': (0.0, 0.8), 'L0_ffn_br': (0.0, 0.1)}
    factors = {}
    for name, (base, spread) in spreads.items():
        noise = np.random.default_rng([zlib.crc32(name.encode()), seed]).standard_normal(out[name].shape)
        drawn = base * np.exp(spread * noise) if base else spread * noise
        out[name] = jnp.asarray(drawn.astype(out[name].dtype))
    for name, factor in factors.items():
        out[name] = (out[name] * factor).astype(out[name].dtype)
    return out
```

```python
from contextlib import ExitStack

import concourse.bass as bass
from concourse import mybir

P = 128
ALU = mybir.AluOpType
ACT = mybir.ActivationFunctionType
AX = mybir.AxisListType
F32 = mybir.dt.float32
F16 = mybir.dt.float16
BF16 = mybir.dt.bfloat16
I32 = mybir.dt.int32
U32 = mybir.dt.uint32

BATCH, SEQ, DM = 16, 256, 2048
NH, NG, HD = 32, 8, 64
REP = NH // NG
EXPERTS, RANK = 8, 16
LOWS = EXPERTS * RANK
ROUTED = LOWS + EXPERTS
TPB = SEQ // P
TILES = BATCH * TPB
SLOTS = NH // 2
UNROLL = 4
ITERS = TILES // UNROLL
CH = 512
NCH = DM // CH
DCH = DM // P

EPS = 1e-5
Q_SCALE = 256.0
LEAST = 2.0 ** -40
EXPONENT = 0x7F800000
RSQRT_SEED = 0x5F3759DF
BIG = 3.0e38

LAG_T, LAG_PV = 2, 4
LN_STEPS = 20
ROUTER_STEPS = 7
K_STEPS = 15
W_DOWN, W_ALL = 15, 18

SIDE_EVEN = [(2, "QT", 0), (3, "LT", 0), (4, "FIN", 0), (5, "FIN", 1), (6, "FIN", 2), (7, "FIN", 3),
             (8, "XT", 0), (9, "QT", 1), (10, "XT", 1), (11, "QT", 2), (12, "XT", 2), (13, "QT", 3),
             (14, "XT", 3), (15, "LOW", 0)]
SIDE_ODD = [(0, "KT", 0), (1, "KT", 1), (2, "QT", 0), (3, "LT", 0), (4, "FIN", 0), (5, "FIN", 1),
            (6, "FIN", 2), (7, "FIN", 3), (8, "XT", 0), (9, "QT", 1), (10, "XT", 1), (10, "KT", 2),
            (11, "QT", 2), (12, "XT", 2), (12, "KT", 3), (13, "QT", 3), (14, "XT", 3), (15, "LOW", 0)]
SIDE = [(j, k, task, part) for j in range(UNROLL) for k, task, part in (SIDE_ODD if j % 2 else SIDE_EVEN)]
AHEAD = {"QT": 1, "KT": 1, "XT": -1, "LOW": -1, "LT": -2, "FIN": -2}


def build(nc, x, ctx, mask, wa, wr, wb, br, out):
    with ExitStack() as es:
        def sb(name, shape, dt=F32):
            return es.enter_context(nc.sbuf_tensor(name, shape, dt))

        def bank(name):
            return es.enter_context(nc.psum_tensor(name, [P, 512], F32))

        def sem(name):
            return es.enter_context(nc.semaphore(name))

        x_in = [sb(f"x_in{i}", [P, DM]) for i in range(4)]
        x1 = [sb(f"x1_{i}", [P, DM]) for i in range(4)]
        xn1 = sb("xn1", [P, DM])
        xn2 = sb("xn2", [P, DM])
        q_split = sb("q_split", [P, NH, 2, HD], F16)
        qT = [sb(f"qT{i}", [P, NH, P], F16) for i in range(2)]
        x2_split = sb("x2_split", [P, 2, DM], F16)
        x2T = sb("x2T", [P, NCH, 2, 4, P], F16)
        scores_sb = [sb(f"scores{i}", [P, 2, SEQ]) for i in range(4)]
        neg_max = sb("neg_max", [P, 4, 2])
        probs = [sb(f"probs{i}", [P, TPB, 2, P]) for i in range(4)]
        probs_low = [sb(f"probs_low{i}", [P, TPB, 2, P], F16) for i in range(4)]
        kT = [[sb(f"kT{b}_{part}", [P, NG, SEQ], F16) for part in range(2)] for b in range(2)]
        v_high = [sb(f"v_high{b}", [P, TPB, NG, HD + 2], F16) for b in range(2)]
        v_low = [sb(f"v_low{b}", [P, TPB, NG, HD], F16) for b in range(2)]
        ctx_in = sb("ctx_in", [P, TPB, NG * HD])
        v_scaled = sb("v_scaled", [P, TPB, NG * HD])
        k_twice = sb("k_twice", [P, 2, TPB, NG, 2, HD], F16)
        mask_in = sb("mask_in", [P, TPB, SEQ])
        mask_scaled = [sb(f"mask_scaled{b}", [P, TPB, SEQ]) for b in range(2)]
        w_high = sb("w_high", [P, DCH, ROUTED], F16)
        w_low = sb("w_low", [P, DCH, ROUTED], F16)
        b_high = sb("b_high", [P, DM], F16)
        b_low = sb("b_low", [P, DM], F16)
        routed = sb("routed", [P, LOWS])
        routed_split = sb("routed_split", [P, 2, P], F16)
        routedT = sb("routedT", [P, 2, P], F16)
        ident32 = sb("ident32", [P, P])
        ident16 = sb("ident16", [P, P], F16)
        br_sb = sb("br_sb", [P, EXPERTS])
        logits = sb("logits", [P, EXPERTS])
        gates = sb("gates", [P, EXPERTS])
        gate_sum = sb("gate_sum", [P, 1])
        gate_max = sb("gate_max", [P, 1])
        gate_rec = sb("gate_rec", [P, 2])
        recip = sb("recip", [P, 2, REP])
        ln = [sb(f"ln{i}", [P, NCH * 6 + 8]) for i in range(2)]
        ctx_max = sb("ctx_max", [P, 1])
        ctx_max_all = sb("ctx_max_all", [P, 1])
        ctx_pow = sb("ctx_pow", [P, 5])
        exp_scale = sb("exp_scale", [P, 2])
        v_unscale = sb("v_unscale", [P, 2])
        w_max = sb("w_max", [P, 3])
        w_max_all = sb("w_max_all", [P, 3])
        w_pow = sb("w_pow", [P, 16])

        s_bank = [bank(f"s_bank{i}") for i in range(2)]
        t_bank = [bank(f"t_bank{i}") for i in range(2)]
        o_bank = [bank(f"o_bank{i}") for i in range(2)]
        m_bank = [bank(f"m_bank{i}") for i in range(2)]

        x_loaded = [sem(f"x_loaded{i}") for i in range(4)]
        stored = [sem(f"stored{i}") for i in range(4)]
        ctx_loaded = sem("ctx_loaded")
        mask_loaded = sem("mask_loaded")
        weights_loaded = sem("weights_loaded")
        idents_ready = sem("idents_ready")
        ones_ready = sem("ones_ready")
        scores_ready = sem("scores_ready")
        masked = sem("masked")
        shifted = sem("shifted")
        turned = sem("turned")
        probs_ready = sem("probs_ready")
        rest_ready = sem("rest_ready")
        pv_done = sem("pv_done")
        recip_ready = sem("recip_ready")
        normed = sem("normed")
        added = sem("added")
        ln_step = [sem("ln1_step"), sem("ln2_step")]
        qh_done = sem("qh_done")
        ql_done = sem("ql_done")
        qt_turned = sem("qt_turned")
        qt_moved = sem("qt_moved")
        x2l_done = sem("x2l_done")
        xt_turned = sem("xt_turned")
        xt_moved = sem("xt_moved")
        low_ready = sem("low_ready")
        router_step = sem("router_step")
        router_exp = sem("router_exp")
        lt_turned = sem("lt_turned")
        lt_moved = sem("lt_moved")
        fin_ready = sem("fin_ready")
        fin_added = sem("fin_added")
        k_step = sem("k_step")
        ctx_max_ready = sem("ctx_max_ready")
        v_ready = sem("v_ready")
        kt_turned = sem("kt_turned")
        kt_moved = sem("kt_moved")
        w_step = sem("w_step")
        w_max_ready = sem("w_max_ready")
        gate, pool_gate = sem("gate"), sem("pool_gate")

        def present(it, j, last=TILES):
            return not isinstance(it, int) or 0 <= UNROLL * it + j < last

        def wait_for(eng, semaphore, value):
            if not isinstance(value, int) or value > 0:
                eng.wait_ge(semaphore, value)

        def rows(t):
            return bass.ds(t * P, P) if not isinstance(t, int) else slice(t * P, t * P + P)

        def iterate(eng, slot, tail):
            for j in range(UNROLL):
                for k in range(SLOTS):
                    slot(0, j, k)
            with eng.Fori(1, ITERS - 1) as it:
                for j in range(UNROLL):
                    for k in range(SLOTS):
                        slot(it, j, k)
            for j in range(UNROLL + tail):
                for k in range(SLOTS):
                    slot(ITERS - 1, j, k)

        def pair(j, k, lag):
            n = SLOTS * j + k - lag
            return n // SLOTS, n % SLOTS, n

        def side_bank(j, task, part):
            m = [(a, c, d) for a, _, c, d in SIDE].index((j % UNROLL, task, part))
            return m_bank[m % 2]

        PAIRS = UNROLL * SLOTS
        GROUPS = UNROLL * NG
        CHUNKS = UNROLL * NCH
        BATCHES = UNROLL // TPB

        block = es.enter_context(nc.Block())

        @block.sync
        def _(sp):
            def load_x(it, j):
                t = it * UNROLL + j
                wait_for(sp, added, it * CHUNKS + NCH * (j - 3))
                sp.dma_start(x_in[j % 4][:], x[rows(t), :]).then_inc(x_loaded[j % 4], 16)

            def load_ctx(it, b):
                wait_for(sp, k_step, (it * BATCHES + b - 1) * K_STEPS + 11)
                t = it * BATCHES + b
                src = ctx[bass.ds(t * SEQ, SEQ), :] if not isinstance(t, int) else ctx[t * SEQ:(t + 1) * SEQ, :]
                sp.dma_start(ctx_in[:], src.rearrange("(c p) d -> p c d", p=P)).then_inc(ctx_loaded, 16)

            load_ctx(0, 0)
            sp.dma_start(mask_in[:], mask.rearrange("(c p) t -> p c t", p=P)).then_inc(mask_loaded, 16)
            for j in range(3):
                sp.dma_start(x_in[j][:], x[rows(j), :]).then_inc(x_loaded[j], 16)
            sp.dma_start(x1[3][:].rearrange("p (c n) -> p c n", c=DCH), wa.rearrange("(c p) n -> p c n", p=P)).then_inc(weights_loaded, 16)
            sp.dma_start(x1[1][:, 0:DCH * EXPERTS].rearrange("p (c n) -> p c n", c=DCH), wr.rearrange("(c p) n -> p c n", p=P)).then_inc(weights_loaded, 16)
            sp.dma_start(x1[2][:], wb).then_inc(weights_loaded, 16)
            sp.dma_start(br_sb[:], br).then_inc(weights_loaded, 16)
            load_ctx(0, 1)

            def slot(it, j, k):
                if k == 4 and present(it, j + 3):
                    load_x(it, j + 3)
                if k == 8 and j % 2 == 1 and present(it, j + 3):
                    load_ctx(it, j // 2 + 2)
                if k == 9 and present(it, j - 2):
                    wait_for(sp, fin_added, it * CHUNKS + NCH * (j - 1))
                    t = it * UNROLL + j - 2
                    sp.dma_start(out[rows(t), :], x1[j - 2 & 3][:]).then_inc(stored[j - 2 & 3], 16)

            iterate(sp, slot, 2)
            for j in range(4):
                sp.wait_ge(stored[j], 16 * ITERS)

        @block.tensor
        def _(pe):
            def scores(it, j, k):
                g, batch = k // 2, j // 2 % 2
                if k % 4 == 0:
                    wait_for(pe, qt_moved, it * CHUNKS + NCH * j + k // 4 + 1)
                if j % 2 == 0 and k % 8 == 0:
                    wait_for(pe, kt_moved, (it * BATCHES + j // 2) * 4 + 2 + k // 4)
                wait_for(pe, masked, it * PAIRS + SLOTS * j + k - 1)
                for r in range(2):
                    to = s_bank[k % 2][:, r * SEQ:(r + 1) * SEQ]
                    q = qT[j % 2][:, 2 * k + r, :]
                    pe.matmul(to, q, kT[batch][0][:, g, :], start=True, stop=False)
                    last = pe.matmul(to, q, kT[batch][1][:, g, :], start=False, stop=True)
                last.then_inc(scores_ready, 1)

            def turn(it, n):
                wait_for(pe, shifted, it * PAIRS + n + 1)
                wait_for(pe, probs_ready, it * PAIRS + n - 1)
                for c in range(TPB):
                    for r in range(2):
                        last = pe.transpose(t_bank[n % 2][:, (2 * c + r) * P:(2 * c + r + 1) * P],
                                            scores_sb[n % 4][:, r, c * P:(c + 1) * P], ident32[:])
                last.then_inc(turned, 1)

            def values(it, j, k, n):
                g, batch = k // 2, j // 2 % 2
                wait_for(pe, rest_ready, it * PAIRS + n + 1)
                if j % 2 == 0 and k == 0:
                    wait_for(pe, v_ready, (it * BATCHES + j // 2 + 1) * 2)
                if k % 2 == 0:
                    wait_for(pe, normed, it * GROUPS + NG * j + g - 1)
                for r in range(2):
                    at = (2 * (k % 2) + r) * (HD + 1)
                    to = o_bank[g % 2][:, at:at + HD + 1]
                    for c in range(TPB):
                        high = probs[n % 4][:, c, r, :].bitcast(BF16)[:, 1::2]
                        low = probs_low[n % 4][:, c, r, :]
                        v1 = v_high[batch][:, c, g, 0:HD + 1]
                        pe.matmul(to, high, v1, start=c == 0, stop=False)
                        pe.matmul(to[:, 0:HD], high, v_low[batch][:, c, g, :], start=False, stop=False)
                        last = pe.matmul(to, low, v1, start=False, stop=c == TPB - 1)
                last.then_inc(pv_done, 1)

            def emptied(it, j, task, part):
                if task == "QT":
                    pe.wait_ge(qt_moved, it * CHUNKS + NCH * (j + 1) + part + 1)
                elif task == "KT":
                    pe.wait_ge(kt_moved, (it * BATCHES + j // 2 + 1) * 4 + part + 1)
                elif task == "XT":
                    pe.wait_ge(xt_moved, it * CHUNKS + NCH * (j - 1) + part + 1)
                elif task == "LT":
                    pe.wait_ge(lt_moved, it * UNROLL + j - 1)
                elif task == "LOW":
                    pe.wait_ge(router_step, (it * UNROLL + j - 1) * ROUTER_STEPS + 5)
                else:
                    pe.wait_ge(fin_added, it * CHUNKS + NCH * (j - 2) + part + 1)

            def q_turn(b, it, j, part):
                pe.wait_ge(ql_done, it * CHUNKS + NCH * j + part + 1)
                for h in range(8):
                    last = pe.transpose(b.bitcast(F16)[:, h * P:(h + 1) * P],
                                        q_split[:, 8 * part + h, :, :].rearrange("p a d -> p (a d)"), ident16[:])
                last.then_inc(qt_turned, 1)

            def k_turn(b, it, batch, part):
                pe.wait_ge(k_step, (it * BATCHES + batch) * K_STEPS + (15 if part % 2 else 13))
                for g in range(4):
                    for c in range(TPB):
                        src = k_twice[:, part % 2, c, 4 * (part // 2) + g, :, :].rearrange("p a d -> p (a d)")
                        last = pe.transpose(b.bitcast(F16)[:, (2 * g + c) * P:(2 * g + c + 1) * P], src, ident16[:])
                last.then_inc(kt_turned, 1)

            def side(it, j, task, part, b):
                if task == "QT":
                    q_turn(b, it, j + 1, part)
                elif task == "KT":
                    k_turn(b, it, j // 2 + 1, part)
                elif task == "XT":
                    pe.wait_ge(x2l_done, it * CHUNKS + NCH * (j - 1) + part + 1)
                    for s in range(2):
                        for c in range(4):
                            at = (4 * part + c) * P
                            last = pe.transpose(b.bitcast(F16)[:, (4 * s + c) * P:(4 * s + c + 1) * P],
                                                x2_split[:, s, at:at + P], ident16[:])
                    last.then_inc(xt_turned, 1)
                elif task == "LOW":
                    pe.wait_ge(xt_moved, it * CHUNKS + NCH * j)
                    if isinstance(it, int) and it == 0:
                        pe.wait_ge(w_step, W_DOWN)
                    to = b[:, 0:ROUTED]
                    for c in range(DCH):
                        high, low = x2T[:, c // 4, 0, c % 4, :], x2T[:, c // 4, 1, c % 4, :]
                        pe.matmul(to, high, w_high[:, c, :], start=c == 0, stop=False)
                        pe.matmul(to, high, w_low[:, c, :], start=False, stop=False)
                        last = pe.matmul(to, low, w_high[:, c, :], start=False, stop=c == DCH - 1)
                    last.then_inc(low_ready, 1)
                elif task == "LT":
                    pe.wait_ge(router_step, (it * UNROLL + j - 1) * ROUTER_STEPS)
                    for s in range(2):
                        last = pe.transpose(b.bitcast(F16)[:, s * P:(s + 1) * P], routed_split[:, s, :], ident16[:])
                    last.then_inc(lt_turned, 1)
                else:
                    if part == 0:
                        pe.wait_ge(lt_moved, it * UNROLL + j - 1)
                        if isinstance(it, int) and it == 0:
                            pe.wait_ge(w_step, W_ALL)
                    cols = slice(part * CH, (part + 1) * CH)
                    pe.matmul(b[:], routedT[:, 0, :], b_high[:, cols], start=True, stop=False)
                    pe.matmul(b[:], routedT[:, 0, :], b_low[:, cols], start=False, stop=False)
                    pe.matmul(b[:], routedT[:, 1, :], b_high[:, cols], start=False, stop=True).then_inc(fin_ready, 1)

            def task_present(it, j, task):
                return present(it, j + AHEAD[task])

            def slot(it, j, k):
                if present(it, j):
                    scores(it, j, k)
                jt, kt, n = pair(j, k, LAG_T)
                if present(it, jt):
                    turn(it, n)
                for m, (js, ks, task, part) in enumerate(SIDE + SIDE):
                    if (js, ks) != (j % UNROLL, k) or m >= len(SIDE) or not task_present(it, j, task):
                        continue
                    b = m % 2
                    back = m - 2
                    while back > m - len(SIDE):
                        jb, _, tb, pb = SIDE[back % len(SIDE)]
                        jb += j - j % UNROLL - (UNROLL if back < 0 else 0)
                        if task_present(it, jb, tb):
                            emptied(it, jb, tb, pb)
                            break
                        back -= 2
                    side(it, j, task, part, m_bank[b])
                jv, kv, n = pair(j, k, LAG_PV)
                if present(it, jv):
                    values(it, jv, kv, n)

            pe.wait_ge(idents_ready, 2)
            for part in range(4):
                if part >= 2:
                    pe.wait_ge(kt_moved, part - 1)
                k_turn(m_bank[part % 2], 0, 0, part)
            for part in range(4):
                if part < 2:
                    pe.wait_ge(kt_moved, part + 3)
                else:
                    pe.wait_ge(qt_moved, part - 1)
                q_turn(m_bank[part % 2], 0, 0, part)
            pe.wait_ge(qt_moved, 4)
            iterate(pe, slot, 2)

        @block.vector
        def _(dve):
            def mask_and_max(it, j, k):
                n = SLOTS * j + k
                wait_for(dve, scores_ready, it * PAIRS + n + 1)
                wait_for(dve, turned, it * PAIRS + n - 3)
                if k == 0 and j % 2 == 0:
                    wait_for(dve, k_step, (it * BATCHES + j // 2) * K_STEPS + 9)
                dve.sem_inc(gate, 1)
                for r in range(2):
                    last = dve.tensor_tensor_reduce(
                        scores_sb[n % 4][:, r, :], s_bank[n % 2][:, r * SEQ:(r + 1) * SEQ],
                        mask_scaled[j // 2 % 2][:, j % 2, :], -1.0, BIG, ALU.add, ALU.min,
                        neg_max[:, n % 4, r:r + 1])
                last.then_inc(masked, 1)

            def norm(it, j, g):
                if g == 0:
                    wait_for(dve, stored[j % 4], 16 * (it + j // 4))
                dve.wait_ge(pv_done, it * PAIRS + SLOTS * j + 2 * g + 2)
                o = o_bank[g % 2][:, 0:REP * (HD + 1)].rearrange("p (h d) -> p h d", h=REP)
                rec = recip[:, g % 2, :]
                dve.reciprocal(rec.unsqueeze(2), o[:, :, HD:HD + 1]).then_inc(recip_ready, 1)
                dve.wait_ge(recip_ready, it * GROUPS + NG * j + g + 1)
                to = x1[j % 4][:, g * REP * HD:(g + 1) * REP * HD].rearrange("p (h d) -> p h d", h=REP)
                dve.scalar_tensor_tensor(to, o[:, :, 0:HD], v_unscale[:, j // 2 % 2:j // 2 % 2 + 1],
                                         rec.unsqueeze(2).to_broadcast([P, REP, HD]),
                                         ALU.mult, ALU.mult).then_inc(normed, 1)

            def residual(it, j, c):
                dve.wait_ge(normed, it * GROUPS + NG * j + 2 * c + 2)
                cols = slice(c * CH, (c + 1) * CH)
                dve.tensor_tensor(x1[j % 4][:, cols], x1[j % 4][:, cols], x_in[j % 4][:, cols],
                                  ALU.add).then_inc(added, 1)

            def stats(it, j, c, which):
                src = (x_in, x1)[which][j % 4]
                if which:
                    dve.wait_ge(added, it * CHUNKS + NCH * j + c + 1)
                elif c == 0:
                    dve.wait_ge(x_loaded[j % 4], 16 * (it + 1 + j // 4))
                dve.bn_stats(ln[which][:, 6 * c:6 * c + 6], src[:, c * CH:(c + 1) * CH]).then_inc(ln_step[which], 1)

            def finish_stats(it, j, which):
                s, step, base = ln[which], ln_step[which], (it * UNROLL + j) * LN_STEPS
                at = NCH * 6
                mean, var, ve, y, w, nb = (s[:, at + i:at + i + 1] for i in range(6))
                dve.wait_ge(step, base + 4)
                dve.sem_inc(gate, 1)
                dve.bn_aggr(s[:, at:at + 2], s[:, 0:at]).then_inc(step, 1)
                dve.wait_ge(step, base + 5)
                dve.tensor_scalar(ve, var, EPS, None, ALU.add).then_inc(step, 1)
                dve.wait_ge(step, base + 6)
                dve.tensor_scalar(w.bitcast(I32), ve.bitcast(I32), 1, None, ALU.logical_shift_right).then_inc(step, 1)
                dve.wait_ge(step, base + 7)
                dve.tensor_scalar(y.bitcast(I32), w.bitcast(I32), -1.0, float(RSQRT_SEED), ALU.mult, ALU.add).then_inc(step, 1)
                for r in range(3):
                    dve.wait_ge(step, base + 8 + 3 * r)
                    dve.scalar_tensor_tensor(w, y, ve, y, ALU.mult, ALU.mult).then_inc(step, 1)
                    dve.wait_ge(step, base + 9 + 3 * r)
                    dve.tensor_scalar(w, w, -0.5, 1.5, ALU.mult, ALU.add).then_inc(step, 1)
                    dve.wait_ge(step, base + 10 + 3 * r)
                    dve.scalar_tensor_tensor(y, y, Q_SCALE if r == 2 else 1.0, w, ALU.mult, ALU.mult).then_inc(step, 1)
                dve.wait_ge(step, base + 17)
                dve.scalar_tensor_tensor(nb, mean, -1.0, y, ALU.mult, ALU.mult).then_inc(step, 1)

            def normalise(it, j, which):
                s, step, base = ln[which], ln_step[which], (it * UNROLL + j) * LN_STEPS
                at = NCH * 6
                dve.wait_ge(step, base + 18)
                wait_for(dve, (ql_done, x2l_done)[which], it * CHUNKS + NCH * j)
                dve.tensor_scalar((xn1, xn2)[which][:], (x_in, x1)[which][j % 4][:], s[:, at + 3:at + 4],
                                  s[:, at + 5:at + 6], ALU.mult, ALU.add).then_inc(step, 1 if which else 2)

            def x2_high(it, j):
                dve.wait_ge(ln_step[1], (it * UNROLL + j) * LN_STEPS + 19)
                wait_for(dve, xt_turned, it * CHUNKS + NCH * j)
                dve.tensor_copy(x2_split[:, 0, :], xn2[:]).then_inc(ln_step[1], 1)

            def router_logits(it, j):
                base = (it * UNROLL + j) * ROUTER_STEPS
                b = side_bank(j + 1, "LOW", 0)
                dve.wait_ge(low_ready, it * UNROLL + j + 1)
                dve.scalar_tensor_tensor(logits[:], b[:, LOWS:ROUTED], w_pow[:, 9:10], br_sb[:],
                                         ALU.mult, ALU.add).then_inc(router_step, 1)
                dve.wait_ge(router_step, base + 1)
                dve.tensor_reduce(gate_max[:], logits[:], AX.X, ALU.max, negate=True).then_inc(router_step, 1)

            def router_weigh(it, j):
                base = (it * UNROLL + j) * ROUTER_STEPS
                b = side_bank(j + 1, "LOW", 0)
                dve.wait_ge(router_exp, it * UNROLL + j + 1)
                dve.reciprocal(gate_rec[:, 0:1], gate_sum[:]).then_inc(router_step, 1)
                dve.wait_ge(router_step, base + 3)
                dve.tensor_scalar(gate_rec[:, 1:2], gate_rec[:, 0:1], 2.0 ** -17, None, ALU.mult).then_inc(router_step, 1)
                dve.wait_ge(router_step, base + 4)
                dve.scalar_tensor_tensor(routed[:].rearrange("p (e r) -> p e r", e=EXPERTS),
                                         b[:, 0:LOWS].rearrange("p (e r) -> p e r", e=EXPERTS),
                                         gate_rec[:, 1:2], gates[:].unsqueeze(2).to_broadcast([P, EXPERTS, RANK]),
                                         ALU.mult, ALU.mult).then_inc(router_step, 1)

            def router_split(it, j):
                base = (it * UNROLL + j) * ROUTER_STEPS
                dve.wait_ge(router_step, base + 5)
                wait_for(dve, lt_turned, it * UNROLL + j)
                dve.tensor_copy(routed_split[:, 0, :], routed[:]).then_inc(router_step, 1)
                dve.wait_ge(router_step, base + 6)
                dve.tensor_tensor(routed_split[:, 1, :], routed[:], routed_split[:, 0, :],
                                  ALU.subtract).then_inc(router_step, 1)

            def finish(it, j, c):
                b = side_bank(j + 2, "FIN", c)
                dve.wait_ge(fin_ready, it * CHUNKS + NCH * j + c + 1)
                cols = slice(c * CH, (c + 1) * CH)
                dve.scalar_tensor_tensor(x1[j % 4][:, cols], b[:], w_pow[:, 10:11], x1[j % 4][:, cols],
                                         ALU.mult, ALU.add).then_inc(fin_added, 1)

            def ctx_maximum(it, b):
                dve.wait_ge(ctx_loaded, (it * BATCHES + b + 1) * 16)
                dve.tensor_reduce(ctx_max[:], ctx_in[:], AX.XY, ALU.max, apply_absolute_value=True).then_inc(k_step, 1)

            def ctx_powers(it, b):
                base = (it * BATCHES + b) * K_STEPS
                power, inv, k_scale, m_scale, top = (ctx_pow[:, i:i + 1] for i in range(5))
                dve.wait_ge(ctx_max_ready, it * BATCHES + b + 1)
                dve.tensor_scalar(top, ctx_max_all[:], LEAST, None, ALU.max).then_inc(k_step, 1)
                dve.wait_ge(k_step, base + 2)
                dve.tensor_scalar(power.bitcast(U32), top.bitcast(U32), EXPONENT, None, ALU.bitwise_and).then_inc(k_step, 1)
                dve.wait_ge(k_step, base + 3)
                dve.reciprocal(inv, power).then_inc(k_step, 1)
                dve.wait_ge(k_step, base + 4)
                dve.tensor_scalar(k_scale, inv, 4096.0, None, ALU.mult).then_inc(k_step, 1)
                wait_for(dve, probs_ready, (it * BATCHES + b - 1) * TPB * SLOTS)
                wait_for(dve, normed, (it * BATCHES + b - 1) * TPB * NG)
                wait_for(dve, masked, (it * BATCHES + b - 1) * TPB * SLOTS)
                dve.tensor_scalar(exp_scale[:, b % 2:b % 2 + 1], power, 2.0 ** -23, None, ALU.mult).then_inc(k_step, 1)
                dve.tensor_scalar(v_unscale[:, b % 2:b % 2 + 1], power, 2.0 ** -12, None, ALU.mult).then_inc(k_step, 1)
                dve.tensor_scalar(m_scale, inv, 2.0 ** 23, None, ALU.mult).then_inc(k_step, 1)
                dve.wait_ge(k_step, base + 8)
                dve.tensor_scalar(mask_scaled[b % 2][:], mask_in[:], m_scale, None, ALU.mult).then_inc(k_step, 1)

            def values_high(it, b):
                wait_for(dve, pv_done, (it * BATCHES + b - 1) * TPB * SLOTS)
                wait_for(dve, v_ready, (it * BATCHES + b) * 2)
                k_scale = ctx_pow[:, 2:3]
                src = ctx_in[:].rearrange("p c (g d) -> p (c g) d", g=NG)
                dve.tensor_scalar(v_high[b % 2][:].rearrange("p c g d -> p (c g) d")[:, :, 0:HD], src, k_scale, None,
                                  ALU.mult).then_inc(k_step, 1)
                dve.tensor_scalar(v_scaled[:], ctx_in[:], k_scale, None, ALU.mult).then_inc(k_step, 1)

            def keys_twice(it, b, part):
                base = (it * BATCHES + b) * K_STEPS
                if part == 0:
                    dve.wait_ge(k_step, base + 10)
                    wait_for(dve, kt_turned, (it * BATCHES + b) * 4)
                else:
                    dve.wait_ge(v_ready, (it * BATCHES + b + 1) * 2)
                src = (v_high, v_low)[part][b % 2]
                for c in range(TPB):
                    dve.tensor_copy(k_twice[:, part, c, :, :, :],
                                    src[:, c, :, 0:HD].unsqueeze(2).to_broadcast([P, NG, 2, HD])).then_inc(k_step, 1)

            def weights(m):
                a_in, r_in, b_in = x1[3][:], x1[1][:, 0:DCH * EXPERTS], x1[2][:]
                wh, wl = w_high[:], w_low[:]
                three = lambda ap, n: ap.rearrange("p (c n) -> p c n", c=DCH)
                if m == 0:
                    dve.wait_ge(weights_loaded, 64)
                    for i, w in enumerate((a_in, r_in, b_in)):
                        dve.tensor_reduce(w_max[:, i:i + 1], w, AX.X, ALU.max, apply_absolute_value=True).then_inc(w_step, 1)
                elif m == 1:
                    p = lambda a, b: w_pow[:, a:b]
                    dve.wait_ge(w_max_ready, 1)
                    dve.tensor_scalar(p(0, 3), w_max_all[:], LEAST, None, ALU.max).then_inc(w_step, 1)
                    dve.wait_ge(w_step, 4)
                    dve.tensor_scalar(p(3, 6).bitcast(U32), p(0, 3).bitcast(U32), EXPONENT, None, ALU.bitwise_and).then_inc(w_step, 1)
                    dve.wait_ge(w_step, 5)
                    dve.reciprocal(p(11, 14), p(3, 6)).then_inc(w_step, 1)
                    dve.wait_ge(w_step, 6)
                    dve.tensor_scalar(p(6, 9), p(11, 14), 4096.0, None, ALU.mult).then_inc(w_step, 1)
                    dve.tensor_scalar(p(9, 10), p(4, 5), 2.0 ** -20, None, ALU.mult).then_inc(w_step, 1)
                    dve.tensor_scalar(p(10, 11), p(3, 4), p(5, 6), 2.0 ** -11, ALU.mult, ALU.mult).then_inc(w_step, 1)
                    dve.wait_ge(w_step, 9)
                elif m == 2:
                    dve.tensor_scalar(wh[:, :, 0:LOWS], three(a_in, LOWS), w_pow[:, 6:7], None, ALU.mult).then_inc(w_step, 1)
                    dve.wait_ge(w_step, 10)
                    dve.tensor_scalar(a_in, a_in, w_pow[:, 6:7], None, ALU.mult).then_inc(w_step, 1)
                elif m == 3:
                    dve.wait_ge(w_step, 11)
                    dve.tensor_tensor(wl[:, :, 0:LOWS], three(a_in, LOWS), wh[:, :, 0:LOWS], ALU.subtract).then_inc(w_step, 1)
                elif m == 4:
                    dve.tensor_scalar(wh[:, :, LOWS:ROUTED], three(r_in, EXPERTS), w_pow[:, 7:8], None, ALU.mult).then_inc(w_step, 1)
                    dve.wait_ge(w_step, 13)
                    dve.tensor_scalar(r_in, r_in, w_pow[:, 7:8], None, ALU.mult).then_inc(w_step, 1)
                    dve.wait_ge(w_step, 14)
                    dve.tensor_tensor(wl[:, :, LOWS:ROUTED], three(r_in, EXPERTS), wh[:, :, LOWS:ROUTED], ALU.subtract).then_inc(w_step, 1)
                elif m == 5:
                    dve.tensor_scalar(b_high[:], b_in, w_pow[:, 8:9], None, ALU.mult).then_inc(w_step, 1)
                    dve.wait_ge(w_step, 16)
                    dve.tensor_scalar(b_in, b_in, w_pow[:, 8:9], None, ALU.mult).then_inc(w_step, 1)
                elif m == 6:
                    dve.wait_ge(w_step, 17)
                    dve.tensor_tensor(b_low[:], b_in, b_high[:], ALU.subtract).then_inc(w_step, 1)

            def slot(it, j, k):
                if present(it, j):
                    mask_and_max(it, j, k)
                if k % 2 == 0:
                    jn, kn, _ = pair(j, k, 6)
                    if present(it, jn):
                        g = kn // 2
                        norm(it, jn, g)
                        if g % 2:
                            residual(it, jn, g // 2)
                            stats(it, jn, g // 2, 1)
                if present(it, j - 1):
                    if k == 4:
                        finish_stats(it, j - 1, 1)
                        normalise(it, j - 1, 1)
                    if k == 5:
                        x2_high(it, j - 1)
                if present(it, j - 2):
                    if k == 0:
                        router_logits(it, j - 2)
                    if k == 1:
                        router_weigh(it, j - 2)
                        router_split(it, j - 2)
                    if 5 <= k <= 8:
                        finish(it, j - 2, k - 5)
                if present(it, j + 2):
                    if k in (1, 3, 9, 11):
                        stats(it, j + 2, (1, 3, 9, 11).index(k), 0)
                    if k == 13:
                        finish_stats(it, j + 2, 0)
                    if k == 14:
                        normalise(it, j + 2, 0)
                if j % 2 == 0 and present(it, j + 2):
                    b = j // 2 + 1
                    if k == 2:
                        ctx_maximum(it, b)
                    if k == 7:
                        ctx_powers(it, b)
                    if k == 10:
                        values_high(it, b)
                    if k == 12:
                        keys_twice(it, b, 0)
                    if k == 15:
                        keys_twice(it, b, 1)
                if isinstance(it, int) and it == 0 and j == 0 and 5 <= k < 12:
                    weights(k - 5)

            for b in range(2):
                dve.memset(v_high[b][:, :, :, HD:HD + 2], 1.0).then_inc(ones_ready, 1)
            ctx_maximum(0, 0)
            dve.wait_ge(mask_loaded, 16)
            ctx_powers(0, 0)
            values_high(0, 0)
            for t in (0, 1):
                for c in range(NCH):
                    stats(0, t, c, 0)
                if t == 0:
                    keys_twice(0, 0, 0)
                finish_stats(0, t, 0)
                if t == 0:
                    keys_twice(0, 0, 1)
                normalise(0, t, 0)
            iterate(dve, slot, 2)

        @block.scalar
        def _(act):
            def exponentiate(it, j, n):
                wait_for(act, turned, it * PAIRS + n + 1)
                wait_for(act, pv_done, it * PAIRS + n - 3)
                act.activation(probs[n % 4][:].rearrange("p c r s -> p (c r s)"), t_bank[n % 2][:], ACT.Exp,
                               scale=exp_scale[:, j // 2 % 2:j // 2 % 2 + 1]).then_inc(probs_ready, 1)

            def shift(it, n):
                wait_for(act, masked, it * PAIRS + n + 1)
                for r in range(2):
                    s = scores_sb[n % 4][:, r, :]
                    last = act.activation(s, s, ACT.Identity, bias=neg_max[:, n % 4, r:r + 1], scale=-1.0)
                last.then_inc(shifted, 1)

            def words(ap):
                return ap.bitcast(F32)

            def q_move(b, it, j, part):
                act.wait_ge(qt_turned, it * CHUNKS + NCH * j + part + 1)
                wait_for(act, scores_ready, it * PAIRS + SLOTS * (j - 1))
                act.copy(words(qT[j % 2][:, 8 * part:8 * part + 8, :].rearrange("p h s -> p (h s)")),
                         b[:]).then_inc(qt_moved, 1)

            def k_move(b, it, batch, part):
                act.wait_ge(kt_turned, (it * BATCHES + batch) * 4 + part + 1)
                wait_for(act, scores_ready, (it * BATCHES + batch - 1) * TPB * SLOTS)
                half = 4 * (part // 2)
                act.copy(words(kT[batch % 2][part % 2][:, half:half + 4, :].rearrange("p g t -> p (g t)")),
                         b[:]).then_inc(kt_moved, 1)

            def q_high(it, j, half):
                act.wait_ge(ln_step[0], (it * UNROLL + j + 1) * LN_STEPS)
                wait_for(act, qt_turned, it * CHUNKS + NCH * j)
                hs = slice(half * NH // 2, (half + 1) * NH // 2)
                act.copy(q_split[:, hs, 0, :], xn1[:].rearrange("p (h d) -> p h d", h=NH)[:, hs, :]).then_inc(qh_done, 1)

            def slot(it, j, k):
                je, ke, n = pair(j, k, LAG_T)
                if present(it, je):
                    exponentiate(it, je, n)
                for m, (js, ks, task, part) in enumerate(SIDE):
                    if (js, ks) != (j % UNROLL, k) or not present(it, j + AHEAD[task]):
                        continue
                    b = m_bank[m % 2]
                    if task == "QT":
                        q_move(b, it, j + 1, part)
                    elif task == "KT":
                        k_move(b, it, j // 2 + 1, part)
                    elif task == "XT":
                        act.wait_ge(xt_turned, it * CHUNKS + NCH * (j - 1) + part + 1)
                        wait_for(act, low_ready, it * UNROLL + j - 1)
                        act.copy(words(x2T[:, part, :, :, :].rearrange("p a c s -> p (a c s)")), b[:]).then_inc(xt_moved, 1)
                    elif task == "LT":
                        act.wait_ge(lt_turned, it * UNROLL + j - 1)
                        wait_for(act, fin_ready, it * CHUNKS + NCH * (j - 2))
                        act.copy(words(routedT[:].rearrange("p a s -> p (a s)")), b[:, 0:P]).then_inc(lt_moved, 1)
                if k == 0 and present(it, j - 2):
                    act.wait_ge(router_step, (it * UNROLL + j - 2) * ROUTER_STEPS + 2)
                    act.activation(gates[:], logits[:], ACT.Exp, bias=gate_max[:], accum_out=gate_sum[:]).then_inc(router_exp, 1)
                if present(it, j):
                    shift(it, SLOTS * j + k)
                if k == 15 and present(it, j + 2):
                    q_high(it, j + 2, 0)
                if k == 0 and present(it, j + 1) and not (isinstance(it, int) and it == 0 and j == 0):
                    q_high(it, j + 1, 1)

            for half in range(2):
                q_high(0, 0, half)
            for part in range(4):
                k_move(m_bank[part % 2], 0, 0, part)
            for part in range(4):
                q_move(m_bank[part % 2], 0, 0, part)
            for half in range(2):
                q_high(0, 1, half)
            iterate(act, slot, 2)

        @block.gpsimd
        def _(pool):
            def rest(it, n):
                wait_for(pool, probs_ready, it * PAIRS + n + 1)
                p = probs[n % 4][:].rearrange("p c r s -> p (c r s)")
                pool.tensor_tensor(probs_low[n % 4][:].rearrange("p c r s -> p (c r s)"), p, p.bitcast(BF16)[:, 1::2],
                                   ALU.subtract).then_inc(rest_ready, 1)

            def q_low(it, j, c):
                pool.wait_ge(qh_done, (it * UNROLL + j) * 2 + c // 2 + 1)
                hs = slice(8 * c, 8 * c + 8)
                pool.tensor_tensor(q_split[:, hs, 1, :], xn1[:].rearrange("p (h d) -> p h d", h=NH)[:, hs, :],
                                   q_split[:, hs, 0, :], ALU.subtract).then_inc(ql_done, 1)

            def x2_low(it, j, c):
                pool.wait_ge(ln_step[1], (it * UNROLL + j + 1) * LN_STEPS)
                cols = slice(c * CH, (c + 1) * CH)
                pool.tensor_tensor(x2_split[:, 1, cols], xn2[:, cols], x2_split[:, 0, cols], ALU.subtract).then_inc(x2l_done, 1)

            def ctx_all(it, b):
                pool.wait_ge(k_step, (it * BATCHES + b) * K_STEPS + 1)
                pool.sem_inc(pool_gate, 1)
                pool.partition_all_reduce(ctx_max_all[:], ctx_max[:], P, bass.bass_isa.ReduceOp.max).then_inc(ctx_max_ready, 1)

            def values_low(it, b, c):
                pool.wait_ge(k_step, (it * BATCHES + b) * K_STEPS + 11)
                pool.tensor_tensor(v_low[b % 2][:, c, :, :], v_scaled[:, c, :].rearrange("p (g d) -> p g d", g=NG),
                                   v_high[b % 2][:, c, :, 0:HD], ALU.subtract).then_inc(v_ready, 1)

            def slot(it, j, k):
                jr, kr, n = pair(j, k, LAG_T)
                if present(it, jr):
                    rest(it, n)
                if k in (0, 2, 4, 6) and present(it, j + 1):
                    q_low(it, j + 1, k // 2)
                if k in (7, 9, 11, 13) and present(it, j - 1):
                    x2_low(it, j - 1, (k - 7) // 2)
                if j % 2 == 0 and present(it, j + 2):
                    b = j // 2 + 1
                    if k == 3:
                        ctx_all(it, b)
                    if k in (10, 12):
                        values_low(it, b, (k - 10) // 2)
                if isinstance(it, int) and it == 0 and j == 0 and k == 5:
                    pool.wait_ge(w_step, 3)
                    pool.partition_all_reduce(w_max_all[:], w_max[:], P, bass.bass_isa.ReduceOp.max).then_inc(w_max_ready, 1)

            ones_at = sem("ones_at")
            for i, ident in enumerate((ident32, ident16)):
                pool.memset(ident[:], 0.0).then_inc(ones_at, 1)
                pool.wait_ge(ones_at, i + 1)
                pool.affine_select(out=ident[:], in_=ident[:], compare_op=ALU.not_equal, fill=1.0, base=0,
                                   pattern=[[-1, P]], channel_multiplier=1).then_inc(idents_ready, 1)
            ctx_all(0, 0)
            for c in range(TPB):
                values_low(0, 0, c)
            for c in range(NCH):
                q_low(0, 0, c)
            iterate(pool, slot, 2)


def kernel(x, ctx_1024, mask_SxS2_ff0, L0_ffn_A, L0_ffn_B, L0_ffn_Wr, L0_ffn_br):
    import numpy as np
    import concourse.bacc as bacc
    from concourse.bass_utils import run_bass_kernel_spmd

    h, r, d = L0_ffn_A.shape
    arrays = {
        "x": np.asarray(x).reshape(-1, d),
        "ctx": np.asarray(ctx_1024).reshape(-1, ctx_1024.shape[-1]),
        "mask": np.asarray(mask_SxS2_ff0),
        "wa": np.asarray(L0_ffn_A).reshape(h * r, d).T,
        "wr": np.asarray(L0_ffn_Wr).T,
        "wb": np.asarray(L0_ffn_B).transpose(0, 2, 1).reshape(h * r, d),
        "br": np.broadcast_to(np.asarray(L0_ffn_br), (P, h)),
    }
    arrays = {f"in_{k}": np.ascontiguousarray(a) for k, a in arrays.items()}
    nc = bacc.Bacc("TRN2", target_bir_lowering=False, num_devices=1)
    args = [nc.dram_tensor(k, a.shape, mybir.dt.from_np(a.dtype), kind="ExternalInput").ap() for k, a in arrays.items()]
    out = nc.dram_tensor("out", arrays["in_x"].shape, F32, kind="ExternalOutput").ap()
    build(nc, *args, out)
    got = run_bass_kernel_spmd(nc, [arrays], core_ids=[0]).results[0]["out"]
    return got.reshape(x.shape)
```

```python
from contextlib import ExitStack

import concourse.bass as bass
from concourse import mybir

P = 128
ALU = mybir.AluOpType
ACT = mybir.ActivationFunctionType
AX = mybir.AxisListType
F32 = mybir.dt.float32
F16 = mybir.dt.float16
BF16 = mybir.dt.bfloat16
I32 = mybir.dt.int32
U32 = mybir.dt.uint32

BATCH, SEQ, DM = 16, 256, 2048
NH, NG, HD = 32, 8, 64
REP = NH // NG
EXPERTS, RANK = 8, 16
LOWS = EXPERTS * RANK
ROUTED = LOWS + EXPERTS
TPB = SEQ // P
TILES = BATCH * TPB
SLOTS = NH // 2
UNROLL = 4
ITERS = TILES // UNROLL
CH = 512
NCH = DM // CH
DCH = DM // P

EPS = 1e-5
Q_SCALE = 256.0
LEAST = 2.0 ** -40
EXPONENT = 0x7F800000
RSQRT_SEED = 0x5F3759DF
BIG = 3.0e38

LAG_SHIFT, LAG_T, LAG_PV, LAG_NORM = 1, 3, 6, 8
LN_STEPS = 19
ROUTER_STEPS = 7
K_STEPS = 15
W_DOWN, W_ALL = 15, 18

SIDE_EVEN = [(0, "FIN", 3, 0), (1, "XT", 1, 1), (3, "XT", 2, 0), (5, "XT", 3, 1), (6, "LOW", 0, 0),
             (7, "LOW", 1, 0), (8, "QT", 0, 1), (9, "QT", 1, 0), (11, "QT", 2, 1), (12, "LT", 0, 0),
             (13, "QT", 3, 1), (13, "FIN", 0, 0), (14, "FIN", 1, 1), (15, "FIN", 2, 0), (15, "XT", 0, 1)]
SIDE_ODD = [(0, "FIN", 3, 0), (1, "XT", 1, 1), (3, "XT", 2, 0), (5, "XT", 3, 1), (6, "LOW", 0, 0),
            (7, "LOW", 1, 0), (8, "QT", 0, 1), (9, "KT", 0, 0), (9, "QT", 1, 1), (10, "KT", 1, 0),
            (11, "QT", 2, 1), (11, "KT", 2, 0), (12, "LT", 0, 1), (13, "QT", 3, 0), (13, "FIN", 0, 1),
            (14, "FIN", 1, 0), (14, "KT", 3, 1), (15, "FIN", 2, 0), (15, "XT", 0, 1)]
SIDE = [(j, *entry) for j in range(UNROLL) for entry in (SIDE_ODD if j % 2 else SIDE_EVEN)]


def ahead(task, part):
    return {"QT": 1, "KT": 1, "XT": -2 if part else -1, "LOW": -2, "LT": -2, "FIN": -3 if part == 3 else -2}[task]


DVE_SIDE = [
    [("REC",), ("NORM",), ("LN1", 10), ("FIN", 2), ("LN1", 11)],
    [("LN1", 12), ("FIN", 3), ("LN1", 13), ("XN1",)],
    [("REC",), ("NORM",), ("BN1", 0), ("RES",)],
    [("BN2",), ("BN1", 1), ("KMAX", 0)],
    [("REC",), ("NORM",), ("BN1", 2)],
    [("BN1", 3), ("K", 0, 0), ("DUP", 1, 0)],
    [("REC",), ("NORM",), ("K", 0, 1), ("RES",), ("K", 0, 2)],
    [("BN2",), ("K", 0, 3), ("LN2", 0), ("K", 0, 4), ("LN2", 1), ("K", 0, 5), ("DUP", 1, 1), ("LN2", 2), ("K", 0, 6)],
    [("REC",), ("R", 0), ("LN2", 3), ("NORM",), ("R", 1), ("LN2", 4), ("K", 0, 7), ("LN2", 5)],
    [("LN2", 6), ("KV", 0, 0), ("LN2", 7), ("R", 2), ("LN2", 8), ("R", 3)],
    [("REC",), ("NORM",), ("LN2", 9), ("R", 4), ("LN2", 10), ("RES",), ("R", 5), ("LN2", 11)],
    [("LN2", 12), ("R", 6), ("LN2", 13), ("LN1", 0), ("XN2",), ("BN2",)],
    [("REC",), ("NORM",), ("LN1", 1), ("KV", 0, 1), ("LN1", 2)],
    [("LN1", 3), ("LN1", 4), ("LN1", 5)],
    [("REC",), ("NORM",), ("LN1", 6), ("FIN", 0), ("RES",), ("LN1", 7)],
    [("BN2",), ("LN1", 8), ("FIN", 1), ("LN1", 9)],
]


def build(nc, x, ctx, mask, wa, wr, wb, br, out):
    with ExitStack() as es:
        def sb(name, shape, dt=F32):
            return es.enter_context(nc.sbuf_tensor(name, shape, dt))

        def bank(name):
            return es.enter_context(nc.psum_tensor(name, [P, 512], F32))

        def sem(name):
            return es.enter_context(nc.semaphore(name))

        x_in = [sb(f"x_in{i}", [P, DM]) for i in range(4)]
        x1 = [sb(f"x1_{i}", [P, DM]) for i in range(4)]
        xn1 = sb("xn1", [P, DM])
        xn2 = sb("xn2", [P, DM])
        q_split = sb("q_split", [P, NH, 2, HD], F16)
        qT = [sb(f"qT{i}", [P, NH, P], F16) for i in range(2)]
        x2_split = sb("x2_split", [P, 2, DM], F16)
        x2T = sb("x2T", [P, NCH, 2, 4, P], F16)
        scores_sb = [sb(f"scores{i}", [P, 2, SEQ]) for i in range(4)]
        low_sb = sb("low_sb", [P, ROUTED])
        neg_max = sb("neg_max", [P, 4, 2])
        probs = [sb(f"probs{i}", [P, TPB, 2, P]) for i in range(4)]
        probs_low = [sb(f"probs_low{i}", [P, TPB, 2, P], F16) for i in range(4)]
        kT = [[sb(f"kT{b}_{part}", [P, NG, SEQ], F16) for part in range(2)] for b in range(2)]
        v_high = [sb(f"v_high{b}", [P, TPB, NG, HD + 2], F16) for b in range(2)]
        v_low = [sb(f"v_low{b}", [P, TPB, NG, HD], F16) for b in range(2)]
        ctx_in = sb("ctx_in", [P, TPB, NG * HD])
        v_scaled = sb("v_scaled", [P, TPB, NG * HD])
        k_twice = sb("k_twice", [P, 2, TPB, NG, 2, HD], F16)
        mask_in = sb("mask_in", [P, TPB, SEQ])
        mask_scaled = [sb(f"mask_scaled{b}", [P, TPB, SEQ]) for b in range(2)]
        w_high = sb("w_high", [P, DCH, ROUTED], F16)
        w_low = sb("w_low", [P, DCH, ROUTED], F16)
        b_high = sb("b_high", [P, DM], F16)
        b_low = sb("b_low", [P, DM], F16)
        routed = sb("routed", [P, LOWS])
        routed_split = sb("routed_split", [P, 2, P], F16)
        routedT = sb("routedT", [P, 2, P], F16)
        ident32 = sb("ident32", [P, P])
        ident16 = sb("ident16", [P, P], F16)
        br_sb = sb("br_sb", [P, EXPERTS])
        logits = sb("logits", [P, EXPERTS])
        gates = sb("gates", [P, EXPERTS])
        gate_sum = sb("gate_sum", [P, 1])
        gate_max = sb("gate_max", [P, 1])
        gate_rec = sb("gate_rec", [P, 2])
        recip = sb("recip", [P, 2, REP])
        ln = [sb(f"ln{i}", [P, NCH * 6 + 8]) for i in range(2)]
        ctx_max = sb("ctx_max", [P, 1])
        ctx_max_all = sb("ctx_max_all", [P, 1])
        ctx_pow = sb("ctx_pow", [P, 5])
        exp_scale = sb("exp_scale", [P, 2])
        v_unscale = sb("v_unscale", [P, 2])
        w_max = sb("w_max", [P, 3])
        w_max_all = sb("w_max_all", [P, 3])
        w_pow = sb("w_pow", [P, 16])

        s_bank = [bank(f"s_bank{i}") for i in range(2)]
        t_bank = [bank(f"t_bank{i}") for i in range(2)]
        o_bank = [bank(f"o_bank{i}") for i in range(2)]
        m_bank = [bank(f"m_bank{i}") for i in range(2)]

        x_loaded = [sem(f"x_loaded{i}") for i in range(4)]
        stored = [sem(f"stored{i}") for i in range(4)]
        ctx_loaded = sem("ctx_loaded")
        mask_loaded = sem("mask_loaded")
        weights_loaded = sem("weights_loaded")
        idents_ready = sem("idents_ready")
        ones_ready = sem("ones_ready")
        scores_ready = sem("scores_ready")
        masked = sem("masked")
        shifted = sem("shifted")
        turned = sem("turned")
        probs_ready = sem("probs_ready")
        rest_ready = sem("rest_ready")
        pv_done = sem("pv_done")
        recip_ready = sem("recip_ready")
        normed = sem("normed")
        added = sem("added")
        ln_step = [sem("ln1_step"), sem("ln2_step")]
        qh_done = sem("qh_done")
        ql_done = sem("ql_done")
        qt_turned = sem("qt_turned")
        qt_moved = sem("qt_moved")
        x2l_done = sem("x2l_done")
        xt_turned = sem("xt_turned")
        xt_moved = sem("xt_moved")
        x2h_done = sem("x2h_done")
        low_ready = sem("low_ready")
        low_moved = sem("low_moved")
        router_step = sem("router_step")
        router_exp = sem("router_exp")
        lt_turned = sem("lt_turned")
        lt_moved = sem("lt_moved")
        fin_ready = sem("fin_ready")
        fin_added = sem("fin_added")
        k_step = sem("k_step")
        ctx_max_ready = sem("ctx_max_ready")
        v_ready = sem("v_ready")
        kt_turned = sem("kt_turned")
        kt_moved = sem("kt_moved")
        w_step = sem("w_step")
        w_max_ready = sem("w_max_ready")
        gate, pool_gate = sem("gate"), sem("pool_gate")

        def present(it, j, last=TILES):
            return not isinstance(it, int) or 0 <= UNROLL * it + j < last

        def wait_for(eng, semaphore, value):
            if not isinstance(value, int) or value > 0:
                eng.wait_ge(semaphore, value)

        def rows(t):
            return bass.ds(t * P, P) if not isinstance(t, int) else slice(t * P, t * P + P)

        def iterate(eng, slot, tail):
            for j in range(UNROLL):
                for k in range(SLOTS):
                    slot(0, j, k)
            with eng.Fori(1, ITERS - 1) as it:
                for j in range(UNROLL):
                    for k in range(SLOTS):
                        slot(it, j, k)
            for j in range(UNROLL + tail):
                for k in range(SLOTS):
                    slot(ITERS - 1, j, k)

        def pair(j, k, lag):
            n = SLOTS * j + k - lag
            return n // SLOTS, n % SLOTS, n

        def side_bank(j, task, part):
            return next(m_bank[b] for js, _, t, p, b in SIDE if (js, t, p) == (j % UNROLL, task, part))

        PAIRS = UNROLL * SLOTS
        GROUPS = UNROLL * NG
        CHUNKS = UNROLL * NCH
        BATCHES = UNROLL // TPB

        block = es.enter_context(nc.Block())

        @block.sync
        def _(sp):
            def load_x(it, j):
                t = it * UNROLL + j
                wait_for(sp, added, it * CHUNKS + NCH * (j - 3))
                sp.dma_start(x_in[j % 4][:], x[rows(t), :]).then_inc(x_loaded[j % 4], 16)

            def load_ctx(it, b):
                wait_for(sp, k_step, (it * BATCHES + b - 1) * K_STEPS + 11)
                t = it * BATCHES + b
                src = ctx[bass.ds(t * SEQ, SEQ), :] if not isinstance(t, int) else ctx[t * SEQ:(t + 1) * SEQ, :]
                sp.dma_start(ctx_in[:], src.rearrange("(c p) d -> p c d", p=P)).then_inc(ctx_loaded, 16)

            load_ctx(0, 0)
            sp.dma_start(mask_in[:], mask.rearrange("(c p) t -> p c t", p=P)).then_inc(mask_loaded, 16)
            for j in range(3):
                sp.dma_start(x_in[j][:], x[rows(j), :]).then_inc(x_loaded[j], 16)
            sp.dma_start(x1[3][:].rearrange("p (c n) -> p c n", c=DCH), wa.rearrange("(c p) n -> p c n", p=P)).then_inc(weights_loaded, 16)
            sp.dma_start(x1[1][:, 0:DCH * EXPERTS].rearrange("p (c n) -> p c n", c=DCH), wr.rearrange("(c p) n -> p c n", p=P)).then_inc(weights_loaded, 16)
            sp.dma_start(x1[2][:], wb).then_inc(weights_loaded, 16)
            sp.dma_start(br_sb[:], br).then_inc(weights_loaded, 16)
            load_ctx(0, 1)

            def slot(it, j, k):
                if k == 7 and present(it, j + 3):
                    load_x(it, j + 3)
                if k == 1 and j % 2 == 1 and present(it, j + 3):
                    load_ctx(it, j // 2 + 2)
                if k == 2 and present(it, j - 3):
                    wait_for(sp, fin_added, it * CHUNKS + NCH * (j - 2))
                    t = it * UNROLL + j - 3
                    sp.dma_start(out[rows(t), :], x1[(j - 3) % 4][:]).then_inc(stored[(j - 3) % 4], 16)

            iterate(sp, slot, 3)
            for j in range(4):
                sp.wait_ge(stored[j], 16 * ITERS)

        @block.tensor
        def _(pe):
            def scores(it, j, k):
                g, batch = k // 2, j // 2 % 2
                if k % 4 == 0:
                    wait_for(pe, qt_moved, it * CHUNKS + NCH * j + k // 4 + 1)
                if j % 2 == 0 and k % 8 == 0:
                    wait_for(pe, kt_moved, (it * BATCHES + j // 2) * 4 + 2 + k // 4)
                wait_for(pe, masked, it * PAIRS + SLOTS * j + k - 1)
                for r in range(2):
                    to = s_bank[k % 2][:, r * SEQ:(r + 1) * SEQ]
                    q = qT[j % 2][:, 2 * k + r, :]
                    pe.matmul(to, q, kT[batch][0][:, g, :], start=True, stop=False)
                    last = pe.matmul(to, q, kT[batch][1][:, g, :], start=False, stop=True)
                last.then_inc(scores_ready, 1)

            def turn(it, n):
                wait_for(pe, shifted, it * PAIRS + n + 1)
                wait_for(pe, probs_ready, it * PAIRS + n - 1)
                for c in range(TPB):
                    for r in range(2):
                        last = pe.transpose(t_bank[n % 2][:, (2 * c + r) * P:(2 * c + r + 1) * P],
                                            scores_sb[n % 4][:, r, c * P:(c + 1) * P], ident32[:])
                last.then_inc(turned, 1)

            def values(it, j, k, n):
                g, batch = k // 2, j // 2 % 2
                wait_for(pe, rest_ready, it * PAIRS + n + 1)
                if j % 2 == 0 and k == 0:
                    wait_for(pe, v_ready, (it * BATCHES + j // 2 + 1) * 2)
                if k % 2 == 0:
                    wait_for(pe, normed, it * GROUPS + NG * j + g - 1)
                for r in range(2):
                    at = (2 * (k % 2) + r) * (HD + 1)
                    to = o_bank[g % 2][:, at:at + HD + 1]
                    for c in range(TPB):
                        high = probs[n % 4][:, c, r, :].bitcast(BF16)[:, 1::2]
                        low = probs_low[n % 4][:, c, r, :]
                        v1 = v_high[batch][:, c, g, 0:HD + 1]
                        pe.matmul(to, high, v1, start=c == 0, stop=False)
                        pe.matmul(to[:, 0:HD], high, v_low[batch][:, c, g, :], start=False, stop=False)
                        last = pe.matmul(to, low, v1, start=False, stop=c == TPB - 1)
                last.then_inc(pv_done, 1)

            def emptied(it, j, task, part):
                if task == "QT":
                    pe.wait_ge(qt_moved, it * CHUNKS + NCH * j + part + 1)
                elif task == "KT":
                    pe.wait_ge(kt_moved, (it * BATCHES + j // 2) * 4 + part + 1)
                elif task == "XT":
                    pe.wait_ge(xt_moved, it * CHUNKS + NCH * j + part + 1)
                elif task == "LT":
                    pe.wait_ge(lt_moved, it * UNROLL + j + 1)
                elif task == "LOW":
                    pe.wait_ge(low_moved, it * UNROLL + j + 1)
                else:
                    pe.wait_ge(fin_added, it * CHUNKS + NCH * j + part + 1)

            def q_turn(b, it, j, part):
                pe.wait_ge(ql_done, it * CHUNKS + NCH * j + part + 1)
                for h in range(8):
                    last = pe.transpose(b.bitcast(F16)[:, h * P:(h + 1) * P],
                                        q_split[:, 8 * part + h, :, :].rearrange("p a d -> p (a d)"), ident16[:])
                last.then_inc(qt_turned, 1)

            def k_turn(b, it, batch, part):
                pe.wait_ge(k_step, (it * BATCHES + batch) * K_STEPS + (15 if part % 2 else 13))
                for g in range(4):
                    for c in range(TPB):
                        src = k_twice[:, part % 2, c, 4 * (part // 2) + g, :, :].rearrange("p a d -> p (a d)")
                        last = pe.transpose(b.bitcast(F16)[:, (2 * g + c) * P:(2 * g + c + 1) * P], src, ident16[:])
                last.then_inc(kt_turned, 1)

            def side(it, j, task, part, b):
                if task == "QT":
                    q_turn(b, it, j, part)
                elif task == "KT":
                    k_turn(b, it, j // 2, part)
                elif task == "XT":
                    pe.wait_ge(x2l_done, it * CHUNKS + NCH * j + part + 1)
                    for s in range(2):
                        for c in range(4):
                            at = (4 * part + c) * P
                            last = pe.transpose(b.bitcast(F16)[:, (4 * s + c) * P:(4 * s + c + 1) * P],
                                                x2_split[:, s, at:at + P], ident16[:])
                    last.then_inc(xt_turned, 1)
                elif task == "LOW":
                    if part == 0:
                        pe.wait_ge(xt_moved, it * CHUNKS + NCH * (j + 1))
                        if isinstance(it, int) and it == 0:
                            pe.wait_ge(w_step, W_DOWN)
                    to = b[:, 0:ROUTED]
                    for c in range(part * DCH // 2, (part + 1) * DCH // 2):
                        high, low = x2T[:, c // 4, 0, c % 4, :], x2T[:, c // 4, 1, c % 4, :]
                        pe.matmul(to, high, w_high[:, c, :], start=c == 0, stop=False)
                        pe.matmul(to, high, w_low[:, c, :], start=False, stop=False)
                        last = pe.matmul(to, low, w_high[:, c, :], start=False, stop=c == DCH - 1)
                    if part == 1:
                        last.then_inc(low_ready, 1)
                elif task == "LT":
                    pe.wait_ge(router_step, (it * UNROLL + j + 1) * ROUTER_STEPS)
                    for s in range(2):
                        last = pe.transpose(b.bitcast(F16)[:, s * P:(s + 1) * P], routed_split[:, s, :], ident16[:])
                    last.then_inc(lt_turned, 1)
                else:
                    if part == 0:
                        pe.wait_ge(lt_moved, it * UNROLL + j + 1)
                        if isinstance(it, int) and it == 0:
                            pe.wait_ge(w_step, W_ALL)
                    cols = slice(part * CH, (part + 1) * CH)
                    pe.matmul(b[:], routedT[:, 0, :], b_high[:, cols], start=True, stop=False)
                    pe.matmul(b[:], routedT[:, 0, :], b_low[:, cols], start=False, stop=False)
                    pe.matmul(b[:], routedT[:, 1, :], b_high[:, cols], start=False, stop=True).then_inc(fin_ready, 1)

            def bank_holder(it, j, m):
                for back in range(m - 1, m - len(SIDE), -1):
                    js, _, task, part, b = SIDE[back % len(SIDE)]
                    if b != SIDE[m][4]:
                        continue
                    at = js + j - j % UNROLL - (UNROLL if back < 0 else 0) + ahead(task, part)
                    if present(it, at):
                        emptied(it, at, task, part)
                        return

            def slot(it, j, k):
                if present(it, j):
                    scores(it, j, k)
                jt, kt, n = pair(j, k, LAG_T)
                if present(it, jt):
                    turn(it, n)
                for m, (js, ks, task, part, b) in enumerate(SIDE):
                    if (js, ks) == (j % UNROLL, k) and present(it, j + ahead(task, part)):
                        if (task, part) != ("LOW", 1):
                            bank_holder(it, j, m)
                        side(it, j + ahead(task, part), task, part, m_bank[b])
                jv, kv, n = pair(j, k, LAG_PV)
                if present(it, jv):
                    values(it, jv, kv, n)

            pe.wait_ge(idents_ready, 2)
            for part in range(4):
                if part >= 2:
                    pe.wait_ge(kt_moved, part - 1)
                k_turn(m_bank[part % 2], 0, 0, part)
            for part in range(4):
                if part < 2:
                    pe.wait_ge(kt_moved, part + 3)
                else:
                    pe.wait_ge(qt_moved, part - 1)
                q_turn(m_bank[part % 2], 0, 0, part)
            pe.wait_ge(qt_moved, 4)
            iterate(pe, slot, 3)

        @block.vector
        def _(dve):
            def mask_and_max(it, j, k, r):
                n = SLOTS * j + k
                if r == 0:
                    wait_for(dve, scores_ready, it * PAIRS + n + 1)
                    wait_for(dve, turned, it * PAIRS + n - 3)
                    if k == 0 and j % 2 == 0:
                        wait_for(dve, k_step, (it * BATCHES + j // 2) * K_STEPS + 9)
                    dve.sem_inc(gate, 1)
                last = dve.tensor_tensor_reduce(
                    scores_sb[n % 4][:, r, :], s_bank[n % 2][:, r * SEQ:(r + 1) * SEQ],
                    mask_scaled[j // 2 % 2][:, j % 2, :], -1.0, BIG, ALU.add, ALU.min,
                    neg_max[:, n % 4, r:r + 1])
                if r == 1:
                    last.then_inc(masked, 1)

            def sums_reciprocal(it, j, g):
                dve.wait_ge(pv_done, it * PAIRS + SLOTS * j + 2 * g + 2)
                o = o_bank[g % 2][:, 0:REP * (HD + 1)].rearrange("p (h d) -> p h d", h=REP)
                dve.reciprocal(recip[:, g % 2, :].unsqueeze(2), o[:, :, HD:HD + 1]).then_inc(recip_ready, 1)

            def norm(it, j, g):
                if g == 0:
                    wait_for(dve, stored[j % 4], 16 * (it + j // 4))
                o = o_bank[g % 2][:, 0:REP * (HD + 1)].rearrange("p (h d) -> p h d", h=REP)
                dve.wait_ge(recip_ready, it * GROUPS + NG * j + g + 1)
                to = x1[j % 4][:, g * REP * HD:(g + 1) * REP * HD].rearrange("p (h d) -> p h d", h=REP)
                dve.scalar_tensor_tensor(to, o[:, :, 0:HD], v_unscale[:, j // 2 % 2:j // 2 % 2 + 1],
                                         recip[:, g % 2, :].unsqueeze(2).to_broadcast([P, REP, HD]),
                                         ALU.mult, ALU.mult).then_inc(normed, 1)

            def residual(it, j, c):
                dve.wait_ge(normed, it * GROUPS + NG * j + 2 * c + 2)
                cols = slice(c * CH, (c + 1) * CH)
                dve.tensor_tensor(x1[j % 4][:, cols], x1[j % 4][:, cols], x_in[j % 4][:, cols],
                                  ALU.add).then_inc(added, 1)

            def stats(it, j, c, which):
                src = (x_in, x1)[which][j % 4]
                if which:
                    dve.wait_ge(added, it * CHUNKS + NCH * j + c + 1)
                elif c == 0:
                    dve.wait_ge(x_loaded[j % 4], 16 * (it + 1 + j // 4))
                dve.bn_stats(ln[which][:, 6 * c:6 * c + 6], src[:, c * CH:(c + 1) * CH]).then_inc(ln_step[which], 1)

            def ln_op(it, j, which, m):
                s, step, base = ln[which], ln_step[which], (it * UNROLL + j) * LN_STEPS
                at = NCH * 6
                mean, var, ve, y, w, nb = (s[:, at + i:at + i + 1] for i in range(6))
                dve.wait_ge(step, base + 4 + m)
                if m == 0:
                    dve.sem_inc(gate, 1)
                    op = dve.bn_aggr(s[:, at:at + 2], s[:, 0:at])
                elif m == 1:
                    op = dve.tensor_scalar(ve, var, EPS, None, ALU.add)
                elif m == 2:
                    op = dve.tensor_scalar(w.bitcast(I32), ve.bitcast(I32), 1, None, ALU.logical_shift_right)
                elif m == 3:
                    op = dve.tensor_scalar(y.bitcast(I32), w.bitcast(I32), -1.0, float(RSQRT_SEED), ALU.mult, ALU.add)
                elif m == 13:
                    op = dve.scalar_tensor_tensor(nb, mean, -1.0, y, ALU.mult, ALU.mult)
                elif m % 3 == 1:
                    op = dve.scalar_tensor_tensor(w, y, ve, y, ALU.mult, ALU.mult)
                elif m % 3 == 2:
                    op = dve.tensor_scalar(w, w, -0.5, 1.5, ALU.mult, ALU.add)
                else:
                    op = dve.scalar_tensor_tensor(y, y, Q_SCALE if m == 12 else 1.0, w, ALU.mult, ALU.mult)
                op.then_inc(step, 1)

            def normalise(it, j, which):
                s, step, base = ln[which], ln_step[which], (it * UNROLL + j) * LN_STEPS
                at = NCH * 6
                dve.wait_ge(step, base + 18)
                wait_for(dve, (ql_done, x2l_done)[which], it * CHUNKS + NCH * j)
                dve.tensor_scalar((xn1, xn2)[which][:], (x_in, x1)[which][j % 4][:], s[:, at + 3:at + 4],
                                  s[:, at + 5:at + 6], ALU.mult, ALU.add).then_inc(step, 1)

            def router_op(it, j, m):
                base = (it * UNROLL + j) * ROUTER_STEPS
                if m == 0:
                    dve.wait_ge(low_moved, it * UNROLL + j + 1)
                    op = dve.scalar_tensor_tensor(logits[:], low_sb[:, LOWS:ROUTED], w_pow[:, 9:10], br_sb[:],
                                                  ALU.mult, ALU.add)
                elif m == 2:
                    dve.wait_ge(router_exp, it * UNROLL + j + 1)
                    op = dve.reciprocal(gate_rec[:, 0:1], gate_sum[:])
                else:
                    dve.wait_ge(router_step, base + m)
                if m == 1:
                    op = dve.tensor_reduce(gate_max[:], logits[:], AX.X, ALU.max, negate=True)
                elif m == 3:
                    op = dve.tensor_scalar(gate_rec[:, 1:2], gate_rec[:, 0:1], 2.0 ** -17, None, ALU.mult)
                elif m == 4:
                    op = dve.scalar_tensor_tensor(routed[:].rearrange("p (e r) -> p e r", e=EXPERTS),
                                                  low_sb[:, 0:LOWS].rearrange("p (e r) -> p e r", e=EXPERTS),
                                                  gate_rec[:, 1:2], gates[:].unsqueeze(2).to_broadcast([P, EXPERTS, RANK]),
                                                  ALU.mult, ALU.mult)
                elif m == 5:
                    wait_for(dve, lt_turned, it * UNROLL + j)
                    op = dve.tensor_copy(routed_split[:, 0, :], routed[:])
                elif m == 6:
                    op = dve.tensor_tensor(routed_split[:, 1, :], routed[:], routed_split[:, 0, :], ALU.subtract)
                op.then_inc(router_step, 1)

            def finish(it, j, c):
                b = side_bank(j - ahead("FIN", c), "FIN", c)
                dve.wait_ge(fin_ready, it * CHUNKS + NCH * j + c + 1)
                cols = slice(c * CH, (c + 1) * CH)
                dve.scalar_tensor_tensor(x1[j % 4][:, cols], b[:], w_pow[:, 10:11], x1[j % 4][:, cols],
                                         ALU.mult, ALU.add).then_inc(fin_added, 1)

            def ctx_maximum(it, b):
                dve.wait_ge(ctx_loaded, (it * BATCHES + b + 1) * 16)
                dve.tensor_reduce(ctx_max[:], ctx_in[:], AX.XY, ALU.max, apply_absolute_value=True).then_inc(k_step, 1)

            def ctx_op(it, b, m):
                base = (it * BATCHES + b) * K_STEPS
                power, inv, k_scale, m_scale, top = (ctx_pow[:, i:i + 1] for i in range(5))
                before = it * BATCHES + b - 1
                if m == 0:
                    dve.wait_ge(ctx_max_ready, it * BATCHES + b + 1)
                    op = dve.tensor_scalar(top, ctx_max_all[:], LEAST, None, ALU.max)
                else:
                    dve.wait_ge(k_step, base + (7 if m > 6 else min(m + 1, 4)) + (m > 6))
                if m == 1:
                    op = dve.tensor_scalar(power.bitcast(U32), top.bitcast(U32), EXPONENT, None, ALU.bitwise_and)
                elif m == 2:
                    op = dve.reciprocal(inv, power)
                elif m == 3:
                    op = dve.tensor_scalar(k_scale, inv, 4096.0, None, ALU.mult)
                elif m == 4:
                    wait_for(dve, probs_ready, before * TPB * SLOTS)
                    op = dve.tensor_scalar(exp_scale[:, b % 2:b % 2 + 1], power, 2.0 ** -23, None, ALU.mult)
                elif m == 5:
                    wait_for(dve, normed, before * TPB * NG)
                    op = dve.tensor_scalar(v_unscale[:, b % 2:b % 2 + 1], power, 2.0 ** -12, None, ALU.mult)
                elif m == 6:
                    op = dve.tensor_scalar(m_scale, inv, 2.0 ** 23, None, ALU.mult)
                elif m == 7:
                    wait_for(dve, masked, before * TPB * SLOTS)
                    op = dve.tensor_scalar(mask_scaled[b % 2][:], mask_in[:], m_scale, None, ALU.mult)
                op.then_inc(k_step, 1)

            def values_scaled(it, b, m):
                k_scale = ctx_pow[:, 2:3]
                if m == 0:
                    wait_for(dve, pv_done, (it * BATCHES + b - 1) * TPB * SLOTS)
                    src = ctx_in[:].rearrange("p c (g d) -> p (c g) d", g=NG)
                    dve.tensor_scalar(v_high[b % 2][:].rearrange("p c g d -> p (c g) d")[:, :, 0:HD], src, k_scale,
                                      None, ALU.mult).then_inc(k_step, 1)
                else:
                    wait_for(dve, v_ready, (it * BATCHES + b) * 2)
                    dve.tensor_scalar(v_scaled[:], ctx_in[:], k_scale, None, ALU.mult).then_inc(k_step, 1)

            def keys_twice(it, b, part):
                base = (it * BATCHES + b) * K_STEPS
                if part == 0:
                    dve.wait_ge(k_step, base + 10)
                    wait_for(dve, kt_turned, (it * BATCHES + b) * 4)
                else:
                    dve.wait_ge(v_ready, (it * BATCHES + b + 1) * 2)
                src = (v_high, v_low)[part][b % 2]
                for c in range(TPB):
                    dve.tensor_copy(k_twice[:, part, c, :, :, :],
                                    src[:, c, :, 0:HD].unsqueeze(2).to_broadcast([P, NG, 2, HD])).then_inc(k_step, 1)

            def weights(m):
                a_in, r_in, b_in = x1[3][:], x1[1][:, 0:DCH * EXPERTS], x1[2][:]
                wh, wl = w_high[:], w_low[:]
                three = lambda ap, n: ap.rearrange("p (c n) -> p c n", c=DCH)
                if m == 0:
                    dve.wait_ge(weights_loaded, 64)
                    for i, w in enumerate((a_in, r_in, b_in)):
                        dve.tensor_reduce(w_max[:, i:i + 1], w, AX.X, ALU.max, apply_absolute_value=True).then_inc(w_step, 1)
                elif m == 1:
                    p = lambda a, b: w_pow[:, a:b]
                    dve.wait_ge(w_max_ready, 1)
                    dve.tensor_scalar(p(0, 3), w_max_all[:], LEAST, None, ALU.max).then_inc(w_step, 1)
                    dve.wait_ge(w_step, 4)
                    dve.tensor_scalar(p(3, 6).bitcast(U32), p(0, 3).bitcast(U32), EXPONENT, None, ALU.bitwise_and).then_inc(w_step, 1)
                    dve.wait_ge(w_step, 5)
                    dve.reciprocal(p(11, 14), p(3, 6)).then_inc(w_step, 1)
                    dve.wait_ge(w_step, 6)
                    dve.tensor_scalar(p(6, 9), p(11, 14), 4096.0, None, ALU.mult).then_inc(w_step, 1)
                    dve.tensor_scalar(p(9, 10), p(4, 5), 2.0 ** -20, None, ALU.mult).then_inc(w_step, 1)
                    dve.tensor_scalar(p(10, 11), p(3, 4), p(5, 6), 2.0 ** -11, ALU.mult, ALU.mult).then_inc(w_step, 1)
                    dve.wait_ge(w_step, 9)
                elif m == 2:
                    dve.tensor_scalar(wh[:, :, 0:LOWS], three(a_in, LOWS), w_pow[:, 6:7], None, ALU.mult).then_inc(w_step, 1)
                    dve.wait_ge(w_step, 10)
                    dve.tensor_scalar(a_in, a_in, w_pow[:, 6:7], None, ALU.mult).then_inc(w_step, 1)
                elif m == 3:
                    dve.wait_ge(w_step, 11)
                    dve.tensor_tensor(wl[:, :, 0:LOWS], three(a_in, LOWS), wh[:, :, 0:LOWS], ALU.subtract).then_inc(w_step, 1)
                elif m == 4:
                    dve.tensor_scalar(wh[:, :, LOWS:ROUTED], three(r_in, EXPERTS), w_pow[:, 7:8], None, ALU.mult).then_inc(w_step, 1)
                    dve.wait_ge(w_step, 13)
                    dve.tensor_scalar(r_in, r_in, w_pow[:, 7:8], None, ALU.mult).then_inc(w_step, 1)
                    dve.wait_ge(w_step, 14)
                    dve.tensor_tensor(wl[:, :, LOWS:ROUTED], three(r_in, EXPERTS), wh[:, :, LOWS:ROUTED], ALU.subtract).then_inc(w_step, 1)
                elif m == 5:
                    dve.tensor_scalar(b_high[:], b_in, w_pow[:, 8:9], None, ALU.mult).then_inc(w_step, 1)
                    dve.wait_ge(w_step, 16)
                    dve.tensor_scalar(b_in, b_in, w_pow[:, 8:9], None, ALU.mult).then_inc(w_step, 1)
                elif m == 6:
                    dve.wait_ge(w_step, 17)
                    dve.tensor_tensor(b_low[:], b_in, b_high[:], ALU.subtract).then_inc(w_step, 1)

            def side(it, j, k, task, part=None, m=None):
                jn, kn, _ = pair(j, k, LAG_NORM)
                if task in ("REC", "NORM", "RES") and present(it, jn):
                    if task == "REC":
                        sums_reciprocal(it, jn, kn // 2)
                    elif task == "NORM":
                        norm(it, jn, kn // 2)
                    else:
                        residual(it, jn, kn // 4)
                jb, kb, _ = pair(j, k, LAG_NORM + 1)
                if task == "BN2" and present(it, jb):
                    stats(it, jb, kb // 4, 1)
                if task == "LN2" and present(it, j - 1):
                    ln_op(it, j - 1, 1, part)
                if task == "XN2" and present(it, j - 1):
                    normalise(it, j - 1, 1)
                if task == "R" and present(it, j - 2):
                    router_op(it, j - 2, part)
                jf = j - (2 if k > 8 else 3)
                if task == "FIN" and present(it, jf):
                    finish(it, jf, part)
                if task == "BN1" and present(it, j + 2):
                    stats(it, j + 2, part, 0)
                j1 = j + (2 if k > 8 else 1)
                if task == "LN1" and present(it, j1):
                    ln_op(it, j1, 0, part)
                if task == "XN1" and present(it, j1):
                    normalise(it, j1, 0)
                if task in ("KMAX", "K", "KV", "DUP") and part == j % 2 and present(it, j + 2 - j % 2):
                    b = j // 2 + 1
                    if task == "KMAX":
                        ctx_maximum(it, b)
                    elif task == "K":
                        ctx_op(it, b, m)
                    elif task == "KV":
                        values_scaled(it, b, m)
                    else:
                        keys_twice(it, b, m)

            def slot(it, j, k):
                for i, entry in enumerate([None] + DVE_SIDE[k][:1] + [None] + DVE_SIDE[k][1:]):
                    if entry:
                        side(it, j, k, *entry)
                    elif present(it, j):
                        mask_and_max(it, j, k, i // 2)
                if isinstance(it, int) and it == 0 and j == 0 and 5 <= k < 12:
                    weights(k - 5)

            for b in range(2):
                dve.memset(v_high[b][:, :, :, HD:HD + 2], 1.0).then_inc(ones_ready, 1)
            ctx_maximum(0, 0)
            dve.wait_ge(mask_loaded, 16)
            for m in range(8):
                ctx_op(0, 0, m)
            for m in range(2):
                values_scaled(0, 0, m)
            for c in range(NCH):
                stats(0, 0, c, 0)
            keys_twice(0, 0, 0)
            for m in range(14):
                ln_op(0, 0, 0, m)
            normalise(0, 0, 0)
            keys_twice(0, 0, 1)
            for c in range(NCH):
                stats(0, 1, c, 0)
            for m in range(10):
                ln_op(0, 1, 0, m)
            iterate(dve, slot, 3)

        @block.scalar
        def _(act):
            def exponentiate(it, j, n):
                wait_for(act, turned, it * PAIRS + n + 1)
                wait_for(act, pv_done, it * PAIRS + n - 3)
                act.activation(probs[n % 4][:].rearrange("p c r s -> p (c r s)"), t_bank[n % 2][:], ACT.Exp,
                               scale=exp_scale[:, j // 2 % 2:j // 2 % 2 + 1]).then_inc(probs_ready, 1)

            def shift(it, n):
                wait_for(act, masked, it * PAIRS + n + 1)
                for r in range(2):
                    s = scores_sb[n % 4][:, r, :]
                    last = act.activation(s, s, ACT.Identity, bias=neg_max[:, n % 4, r:r + 1], scale=-1.0)
                last.then_inc(shifted, 1)

            def words(ap):
                return ap.bitcast(F32)

            def q_move(b, it, j, part):
                act.wait_ge(qt_turned, it * CHUNKS + NCH * j + part + 1)
                wait_for(act, scores_ready, it * PAIRS + SLOTS * (j - 1))
                act.copy(words(qT[j % 2][:, 8 * part:8 * part + 8, :].rearrange("p h s -> p (h s)")),
                         b[:]).then_inc(qt_moved, 1)

            def k_move(b, it, batch, part):
                act.wait_ge(kt_turned, (it * BATCHES + batch) * 4 + part + 1)
                wait_for(act, scores_ready, (it * BATCHES + batch - 1) * TPB * SLOTS)
                half = 4 * (part // 2)
                act.copy(words(kT[batch % 2][part % 2][:, half:half + 4, :].rearrange("p g t -> p (g t)")),
                         b[:]).then_inc(kt_moved, 1)

            def q_high(it, j, half):
                act.wait_ge(ln_step[0], (it * UNROLL + j + 1) * LN_STEPS)
                wait_for(act, qt_turned, it * CHUNKS + NCH * j)
                hs = slice(half * NH // 2, (half + 1) * NH // 2)
                act.copy(q_split[:, hs, 0, :], xn1[:].rearrange("p (h d) -> p h d", h=NH)[:, hs, :]).then_inc(qh_done, 1)

            def x2_high(it, j, half):
                act.wait_ge(ln_step[1], (it * UNROLL + j + 1) * LN_STEPS)
                wait_for(act, xt_turned, it * CHUNKS + NCH * j)
                cols = slice(half * DM // 2, (half + 1) * DM // 2)
                act.copy(x2_split[:, 0, cols], xn2[:, cols]).then_inc(x2h_done, 1)

            def side(it, j, task, part, b):
                if task == "QT":
                    q_move(b, it, j, part)
                elif task == "KT":
                    k_move(b, it, j // 2, part)
                elif task == "XT":
                    act.wait_ge(xt_turned, it * CHUNKS + NCH * j + part + 1)
                    wait_for(act, low_ready, it * UNROLL + j)
                    act.copy(words(x2T[:, part, :, :, :].rearrange("p a c s -> p (a c s)")), b[:]).then_inc(xt_moved, 1)
                elif task == "LOW" and part == 1:
                    act.wait_ge(low_ready, it * UNROLL + j + 1)
                    wait_for(act, router_step, (it * UNROLL + j) * ROUTER_STEPS)
                    act.copy(low_sb[:], b[:, 0:ROUTED]).then_inc(low_moved, 1)
                elif task == "LT":
                    act.wait_ge(lt_turned, it * UNROLL + j + 1)
                    wait_for(act, fin_ready, it * CHUNKS + NCH * j)
                    act.copy(words(routedT[:].rearrange("p a s -> p (a s)")), b[:, 0:P]).then_inc(lt_moved, 1)

            def slot(it, j, k):
                je, ke, n = pair(j, k, LAG_T)
                if present(it, je):
                    exponentiate(it, je, n)
                for js, ks, task, part, b in SIDE:
                    if (js, ks) == (j % UNROLL, k) and present(it, j + ahead(task, part)):
                        side(it, j + ahead(task, part), task, part, m_bank[b])
                if k == 9 and present(it, j - 2):
                    act.wait_ge(router_step, (it * UNROLL + j - 2) * ROUTER_STEPS + 2)
                    act.activation(gates[:], logits[:], ACT.Exp, bias=gate_max[:], accum_out=gate_sum[:]).then_inc(router_exp, 1)
                js, ks, n = pair(j, k, LAG_SHIFT)
                if present(it, js):
                    shift(it, n)
                if k in (2, 4) and present(it, j + 1):
                    q_high(it, j + 1, (k - 2) // 2)
                if k in (12, 14) and present(it, j - 1):
                    x2_high(it, j - 1, (k - 12) // 2)

            for half in range(2):
                q_high(0, 0, half)
            for part in range(4):
                k_move(m_bank[part % 2], 0, 0, part)
            for part in range(4):
                q_move(m_bank[part % 2], 0, 0, part)
            iterate(act, slot, 3)

        @block.gpsimd
        def _(pool):
            def rest(it, n):
                wait_for(pool, probs_ready, it * PAIRS + n + 1)
                p = probs[n % 4][:].rearrange("p c r s -> p (c r s)")
                pool.tensor_tensor(probs_low[n % 4][:].rearrange("p c r s -> p (c r s)"), p, p.bitcast(BF16)[:, 1::2],
                                   ALU.subtract).then_inc(rest_ready, 1)

            def q_low(it, j, c):
                pool.wait_ge(qh_done, (it * UNROLL + j) * 2 + c // 2 + 1)
                hs = slice(8 * c, 8 * c + 8)
                pool.tensor_tensor(q_split[:, hs, 1, :], xn1[:].rearrange("p (h d) -> p h d", h=NH)[:, hs, :],
                                   q_split[:, hs, 0, :], ALU.subtract).then_inc(ql_done, 1)

            def x2_low(it, j, c):
                pool.wait_ge(x2h_done, (it * UNROLL + j) * 2 + c // 2 + 1)
                cols = slice(c * CH, (c + 1) * CH)
                pool.tensor_tensor(x2_split[:, 1, cols], xn2[:, cols], x2_split[:, 0, cols], ALU.subtract).then_inc(x2l_done, 1)

            def ctx_all(it, b):
                pool.wait_ge(k_step, (it * BATCHES + b) * K_STEPS + 1)
                pool.sem_inc(pool_gate, 1)
                pool.partition_all_reduce(ctx_max_all[:], ctx_max[:], P, bass.bass_isa.ReduceOp.max).then_inc(ctx_max_ready, 1)

            def values_low(it, b, c):
                pool.wait_ge(k_step, (it * BATCHES + b) * K_STEPS + 11)
                pool.tensor_tensor(v_low[b % 2][:, c, :, :], v_scaled[:, c, :].rearrange("p (g d) -> p g d", g=NG),
                                   v_high[b % 2][:, c, :, 0:HD], ALU.subtract).then_inc(v_ready, 1)

            def slot(it, j, k):
                jr, kr, n = pair(j, k, LAG_T)
                if present(it, jr):
                    rest(it, n)
                if k in (5, 7, 9, 11) and present(it, j + 1):
                    q_low(it, j + 1, (k - 5) // 2)
                if k in (13, 15) and present(it, j - 1):
                    x2_low(it, j - 1, (k - 13) // 2)
                if k in (1, 3) and present(it, j - 2):
                    x2_low(it, j - 2, (k + 3) // 2)
                if j % 2 == 0 and k == 4 and present(it, j + 2):
                    ctx_all(it, j // 2 + 1)
                if j % 2 == 0 and k == 14 and present(it, j + 2):
                    values_low(it, j // 2 + 1, 0)
                if j % 2 == 1 and k == 0 and present(it, j + 1):
                    values_low(it, j // 2 + 1, 1)
                if isinstance(it, int) and it == 0 and j == 0 and k == 5:
                    pool.wait_ge(w_step, 3)
                    pool.partition_all_reduce(w_max_all[:], w_max[:], P, bass.bass_isa.ReduceOp.max).then_inc(w_max_ready, 1)

            ones_at = sem("ones_at")
            for i, ident in enumerate((ident32, ident16)):
                pool.memset(ident[:], 0.0).then_inc(ones_at, 1)
                pool.wait_ge(ones_at, i + 1)
                pool.affine_select(out=ident[:], in_=ident[:], compare_op=ALU.not_equal, fill=1.0, base=0,
                                   pattern=[[-1, P]], channel_multiplier=1).then_inc(idents_ready, 1)
            ctx_all(0, 0)
            for c in range(TPB):
                values_low(0, 0, c)
            for c in range(NCH):
                q_low(0, 0, c)
            iterate(pool, slot, 3)


def kernel(x, ctx_1024, mask_SxS2_ff0, L0_ffn_A, L0_ffn_B, L0_ffn_Wr, L0_ffn_br):
    import numpy as np
    import concourse.bacc as bacc
    from concourse.bass_utils import run_bass_kernel_spmd

    h, r, d = L0_ffn_A.shape
    arrays = {
        "x": np.asarray(x).reshape(-1, d),
        "ctx": np.asarray(ctx_1024).reshape(-1, ctx_1024.shape[-1]),
        "mask": np.asarray(mask_SxS2_ff0),
        "wa": np.asarray(L0_ffn_A).reshape(h * r, d).T,
        "wr": np.asarray(L0_ffn_Wr).T,
        "wb": np.asarray(L0_ffn_B).transpose(0, 2, 1).reshape(h * r, d),
        "br": np.broadcast_to(np.asarray(L0_ffn_br), (P, h)),
    }
    arrays = {f"in_{k}": np.ascontiguousarray(a) for k, a in arrays.items()}
    nc = bacc.Bacc("TRN2", target_bir_lowering=False, num_devices=1)
    args = [nc.dram_tensor(k, a.shape, mybir.dt.from_np(a.dtype), kind="ExternalInput").ap() for k, a in arrays.items()]
    out = nc.dram_tensor("out", arrays["in_x"].shape, F32, kind="ExternalOutput").ap()
    build(nc, *args, out)
    got = run_bass_kernel_spmd(nc, [arrays], core_ids=[0]).results[0]["out"]
    return got.reshape(x.shape)
```

```python
from contextlib import ExitStack

import concourse.bass as bass
from concourse import mybir

P = 128
ALU = mybir.AluOpType
ACT = mybir.ActivationFunctionType
AX = mybir.AxisListType
F32 = mybir.dt.float32
F16 = mybir.dt.float16
BF16 = mybir.dt.bfloat16
I32 = mybir.dt.int32
U32 = mybir.dt.uint32

BATCH, SEQ, DM = 16, 256, 2048
NH, NG, HD = 32, 8, 64
REP = NH // NG
EXPERTS, RANK = 8, 16
LOWS = EXPERTS * RANK
ROUTED = LOWS + EXPERTS
TPB = SEQ // P
TILES = BATCH * TPB
SLOTS = NH // 2
UNROLL = 4
ITERS = TILES // UNROLL
CH = 512
NCH = DM // CH
DCH = DM // P

EPS = 1e-5
Q_SCALE = 256.0
LEAST = 2.0 ** -40
EXPONENT = 0x7F800000
RSQRT_SEED = 0x5F3759DF
BIG = 3.0e38

LAG_SHIFT, LAG_T, LAG_EXP, LAG_REST, LAG_PV = 1, 3, 3, 4, 6
RING = 8
LN_STEPS = 15
ROUTER_STEPS = 6
K_STEPS = 15
W_DOWN, W_ALL = 15, 18

PE_SLOTS = [
    [(-3, "FIN", 2), "SCORES", (-2, "XT", 0), "TURN", "VALUES"],
    ["SCORES", "TURN", "VALUES", (-2, "XT", 1)],
    ["SCORES", "TURN", "VALUES"],
    ["SCORES", (-3, "FIN", 3), "TURN", "VALUES"],
    ["SCORES", "TURN", (-2, "XT", 2), "VALUES", (-2, "XT", 3)],
    ["SCORES", "TURN", "VALUES"],
    ["SCORES", "TURN", "VALUES"],
    ["SCORES", "TURN", "VALUES", (-2, "LOW", 0)],
    [(-2, "LOW", 1), "SCORES", "TURN", "VALUES"],
    ["SCORES", (1, "QT", 0), (1, "KT", 0), "TURN", "VALUES"],
    [(1, "QT", 1), "SCORES", "TURN", "VALUES"],
    [(1, "KT", 1), "SCORES", (1, "QT", 2), "TURN", "VALUES"],
    [(1, "KT", 2), "SCORES", "TURN", (1, "KT", 3), "VALUES"],
    [(1, "QT", 3), "SCORES", "TURN", "VALUES", (-2, "LT", 0)],
    ["SCORES", "TURN", "VALUES", (-2, "FIN", 0), (-2, "FIN", 1)],
    ["SCORES", "TURN", "VALUES"],
]
DVE_SLOTS = [
    [(-1, "NORM", 4), "MASK0", "MASK1", (2, "BN1", 0)],
    ["MASK0", "MASK1"],
    [(2, "BN1", 1), (-1, "REC", 5), (-2, "XTL", 0), "MASK0", "MASK1", (-1, "NORM", 5)],
    ["MASK0", (-2, "XTL", 1), (-3, "FIN", 3), "MASK1", (-1, "REC", 6), (-1, "BN2", 1)],
    ["MASK0", (2, "BN1", 2), "MASK1", (-1, "NORM", 6)],
    ["MASK0", "MASK1", (2, "KMAX", 0), (-2, "XTL", 2)],
    [(-2, "XTL", 3), (2, "BN1", 3), "MASK0", (-1, "REC", 7), (1, "DUP", 0), "MASK1", (-1, "NORM", 7)],
    ["MASK0", (0, "LN", 0), (2, "KOP", 0), (-1, "BN2", 2), "MASK1"],
    [(2, "KOP", 1), (-1, "BN2", 3), (0, "REC", 0), "MASK0", "MASK1", (2, "KOP", 2), (2, "KOP", 3), (0, "LN", 1),
     (0, "NORM", 0)],
    ["MASK0", (0, "LN", 2), (2, "KOP", 4), (-2, "R", 0), (0, "LN", 3), (2, "KOP", 5), "MASK1", (-2, "R", 1),
     (0, "LN", 4)],
    [(1, "DUP", 1), "MASK0", (0, "LN", 5), (0, "REC", 1), (2, "KOP", 6), (0, "LN", 6), "MASK1", (0, "NORM", 1),
     (2, "KOP", 7), (0, "LN", 7), (-2, "R", 2), (2, "KV", 0), (0, "LN", 8)],
    [(-2, "R", 3), "MASK0", (-2, "R", 4), "MASK1", (0, "REC", 2)],
    [(0, "LN", 9), (-2, "R", 5), "MASK0", (0, "LN", 10), "MASK1", (2, "KV", 1)],
    [(0, "LN", 11), (0, "LN", 12), (0, "LN", 13), (0, "NORM", 2), (0, "LN", 14), "MASK0", (-1, "XN2", 0),
     (0, "REC", 3), "MASK1"],
    [(-1, "XN2", 1), "MASK0", (0, "NORM", 3), "MASK1", (-2, "FIN", 0), (-2, "FIN", 1)],
    [(0, "BN2", 0), (0, "REC", 4), "MASK0", "MASK1", (-2, "FIN", 2)],
]
ACT_SLOTS = [
    ["EXP", "SHIFT"],
    ["EXP", "SHIFT", (-2, "XT", 1)],
    ["EXP", "SHIFT"],
    ["EXP", "SHIFT"],
    ["EXP", (-2, "XT", 2), "SHIFT", (-2, "XT", 3)],
    ["EXP", "SHIFT", (1, "XN1", 1)],
    ["EXP", "SHIFT", (1, "QH", 1)],
    ["EXP", "SHIFT"],
    [(-2, "LOW", 1), "EXP", "SHIFT", (1, "QT", 0), (1, "KT", 0)],
    ["EXP", "SHIFT"],
    [(1, "QT", 1), "EXP", (1, "KT", 1), (-2, "REXP", 0), "SHIFT"],
    ["EXP", (1, "QT", 2), (1, "KT", 2), "SHIFT"],
    [(1, "KT", 3), "EXP", "SHIFT", (1, "QT", 3)],
    [(-2, "LT", 0), "EXP", "SHIFT"],
    [(2, "XN1", 0), "EXP", "SHIFT"],
    ["EXP", "SHIFT", (-1, "XT", 0), (2, "QH", 0)],
]
POOL_SLOTS = [
    ["REST"],
    ["REST", (1, "QL", 0)],
    ["REST"],
    ["REST", (1, "QL", 1)],
    ["REST"],
    ["REST", (-1, "RES", 2)],
    [(2, "KALL", 0), "REST"],
    [(-1, "RES", 3), "REST"],
    ["REST", (1, "VL", 1)],
    [(1, "QL", 2), "REST"],
    ["REST"],
    [(1, "QL", 3), "REST"],
    ["REST"],
    ["REST", (0, "RES", 0)],
    ["REST", (2, "VL", 0), (0, "RES", 1)],
    ["REST"],
]
OF_BATCH = ("KT", "KMAX", "KOP", "KV", "DUP", "KALL", "VL")
EARLY, DRAIN = 2, 3


def side_banks():
    tasks, bank = [], 1
    for j in range(UNROLL):
        for entries in PE_SLOTS:
            for e in entries:
                if isinstance(e, tuple) and not (e[1] in OF_BATCH and (j + e[0]) % TPB):
                    bank = bank if e[1:] == ("LOW", 1) else 1 - bank
                    tasks.append((j, *e, bank))
    return tasks


def build(nc, x, ctx, mask, wa, wr, wb, br, out):
    with ExitStack() as es:
        def sb(name, shape, dt=F32):
            return es.enter_context(nc.sbuf_tensor(name, shape, dt))

        def bank(name):
            return es.enter_context(nc.psum_tensor(name, [P, 512], F32))

        def sem(name):
            return es.enter_context(nc.semaphore(name))

        x_in = [sb(f"x_in{i}", [P, DM]) for i in range(4)]
        x1 = [sb(f"x1_{i}", [P, DM]) for i in range(4)]
        xn1 = sb("xn1", [P, DM])
        xn2 = sb("xn2", [P, DM])
        q_split = sb("q_split", [P, NH, 2, HD], F16)
        qT = [sb(f"qT{i}", [P, NH, P], F16) for i in range(2)]
        x2T = sb("x2T", [P, NCH, 2, 4, P], F16)
        scores_sb = [sb(f"scores{i}", [P, 2, SEQ]) for i in range(4)]
        low_sb = sb("low_sb", [P, ROUTED])
        neg_max = sb("neg_max", [P, 4, 2])
        probs = [sb(f"probs{i}", [P, TPB, 2, P]) for i in range(RING)]
        probs_low = [sb(f"probs_low{i}", [P, TPB, 2, P], F16) for i in range(RING)]
        kT = [[sb(f"kT{b}_{part}", [P, NG, SEQ], F16) for part in range(2)] for b in range(2)]
        v_high = [sb(f"v_high{b}", [P, TPB, NG, HD + 2], F16) for b in range(2)]
        v_low = [sb(f"v_low{b}", [P, TPB, NG, HD], F16) for b in range(2)]
        ctx_in = sb("ctx_in", [P, TPB, NG * HD])
        k_twice = sb("k_twice", [P, 2, TPB, NG, 2, HD], F16)
        mask_in = sb("mask_in", [P, TPB, SEQ])
        mask_scaled = [sb(f"mask_scaled{b}", [P, TPB, SEQ]) for b in range(2)]
        w_high = sb("w_high", [P, DCH, ROUTED], F16)
        w_low = sb("w_low", [P, DCH, ROUTED], F16)
        b_high = sb("b_high", [P, DM], F16)
        b_low = sb("b_low", [P, DM], F16)
        routed = sb("routed", [P, LOWS])
        routed_split = sb("routed_split", [P, 2, P], F16)
        routedT = sb("routedT", [P, 2, P], F16)
        ident32 = sb("ident32", [P, P])
        ident16 = sb("ident16", [P, P], F16)
        br_sb = sb("br_sb", [P, EXPERTS])
        logits = sb("logits", [P, EXPERTS])
        gates = sb("gates", [P, EXPERTS])
        gate_sum = sb("gate_sum", [P, 1])
        gate_max = sb("gate_max", [P, 1])
        gate_rec = sb("gate_rec", [P, 1])
        recip = sb("recip", [P, 2, REP])
        ln_stats = [sb(f"ln{i}_stats", [P, NCH * 6]) for i in range(2)]
        ln_mv = sb("ln_mv", [P, 2, 2])
        ln_work = sb("ln_work", [P, 4, 2])
        ctx_max = sb("ctx_max", [P, 1])
        ctx_max_all = sb("ctx_max_all", [P, 1])
        ctx_pow = sb("ctx_pow", [P, 5])
        exp_scale = sb("exp_scale", [P, 2])
        v_unscale = sb("v_unscale", [P, 2])
        w_max = sb("w_max", [P, 3])
        w_max_all = sb("w_max_all", [P, 3])
        w_pow = sb("w_pow", [P, 16])

        s_bank = [bank(f"s_bank{i}") for i in range(2)]
        t_bank = [bank(f"t_bank{i}") for i in range(2)]
        o_bank = [bank(f"o_bank{i}") for i in range(2)]
        m_bank = [bank(f"m_bank{i}") for i in range(2)]

        x_loaded = [sem(f"x_loaded{i}") for i in range(4)]
        stored = [sem(f"stored{i}") for i in range(4)]
        ctx_loaded = sem("ctx_loaded")
        mask_loaded = sem("mask_loaded")
        weights_loaded = sem("weights_loaded")
        idents_ready = sem("idents_ready")
        ones_ready = sem("ones_ready")
        scores_ready = sem("scores_ready")
        masked = sem("masked")
        shifted = sem("shifted")
        turned = sem("turned")
        probs_ready = sem("probs_ready")
        rest_ready = sem("rest_ready")
        pv_done = sem("pv_done")
        recip_ready = sem("recip_ready")
        normed = sem("normed")
        added = sem("added")
        stats_done = [sem("stats1_done"), sem("stats2_done")]
        ln_step = sem("ln_step")
        normalised = [sem("normalised1"), sem("normalised2")]
        qh_done = sem("qh_done")
        ql_done = sem("ql_done")
        qt_turned = sem("qt_turned")
        qt_moved = sem("qt_moved")
        xt_turned = sem("xt_turned")
        xt_high = sem("xt_high")
        xt_low = sem("xt_low")
        low_ready = sem("low_ready")
        low_moved = sem("low_moved")
        router_step = sem("router_step")
        router_exp = sem("router_exp")
        lt_turned = sem("lt_turned")
        lt_moved = sem("lt_moved")
        fin_ready = sem("fin_ready")
        fin_added = sem("fin_added")
        k_step = sem("k_step")
        ctx_max_ready = sem("ctx_max_ready")
        v_ready = sem("v_ready")
        kt_turned = sem("kt_turned")
        kt_moved = sem("kt_moved")
        w_step = sem("w_step")
        w_max_ready = sem("w_max_ready")
        gate, pool_gate = sem("gate"), sem("pool_gate")

        def present(it, j, last=TILES):
            return not isinstance(it, int) or 0 <= UNROLL * it + j < last

        def wait_for(eng, semaphore, value):
            if not isinstance(value, int) or value > 0:
                eng.wait_ge(semaphore, value)

        def rows(t):
            return bass.ds(t * P, P) if not isinstance(t, int) else slice(t * P, t * P + P)

        def iterate(eng, slot):
            for j in range(-EARLY, UNROLL):
                for k in range(SLOTS):
                    slot(0, j, k)
            with eng.Fori(1, ITERS - 1) as it:
                for j in range(UNROLL):
                    for k in range(SLOTS):
                        slot(it, j, k)
            for j in range(UNROLL + DRAIN):
                for k in range(SLOTS):
                    slot(ITERS - 1, j, k)

        def pair(j, k, lag):
            n = SLOTS * j + k - lag
            return n // SLOTS, n % SLOTS, n

        def side_tile(it, j, entry):
            at = j + entry[0]
            if not present(it, at) or (entry[1] in OF_BATCH and at % TPB):
                return None
            return at

        side_tasks = side_banks()

        def side_bank(at, task, part):
            return next(m_bank[b] for js, d, t, p, b in side_tasks if (t, p) == (task, part) and (js + d - at) % UNROLL == 0)

        PAIRS = UNROLL * SLOTS
        GROUPS = UNROLL * NG
        CHUNKS = UNROLL * NCH
        BATCHES = UNROLL // TPB

        block = es.enter_context(nc.Block())

        @block.sync
        def _(sp):
            def load_x(it, j):
                t = it * UNROLL + j
                wait_for(sp, added, it * CHUNKS + NCH * (j - 3))
                sp.dma_start(x_in[j % 4][:], x[rows(t), :]).then_inc(x_loaded[j % 4], 16)

            def load_ctx(it, b):
                wait_for(sp, v_ready, (it * BATCHES + b) * 2)
                t = it * BATCHES + b
                src = ctx[bass.ds(t * SEQ, SEQ), :] if not isinstance(t, int) else ctx[t * SEQ:(t + 1) * SEQ, :]
                sp.dma_start(ctx_in[:], src.rearrange("(c p) d -> p c d", p=P)).then_inc(ctx_loaded, 16)

            sp.dma_start(x_in[0][:], x[rows(0), :]).then_inc(x_loaded[0], 16)
            load_ctx(0, 0)
            sp.dma_start(mask_in[:], mask.rearrange("(c p) t -> p c t", p=P)).then_inc(mask_loaded, 16)
            for j in range(1, 3):
                sp.dma_start(x_in[j][:], x[rows(j), :]).then_inc(x_loaded[j], 16)
            sp.dma_start(x1[3][:].rearrange("p (c n) -> p c n", c=DCH), wa.rearrange("(c p) n -> p c n", p=P)).then_inc(weights_loaded, 16)
            sp.dma_start(x1[1][:, 0:DCH * EXPERTS].rearrange("p (c n) -> p c n", c=DCH), wr.rearrange("(c p) n -> p c n", p=P)).then_inc(weights_loaded, 16)
            sp.dma_start(x1[2][:], wb).then_inc(weights_loaded, 16)
            sp.dma_start(br_sb[:], br).then_inc(weights_loaded, 16)
            load_ctx(0, 1)

            def slot(it, j, k):
                if k == 7 and j >= 0 and present(it, j + 3):
                    load_x(it, j + 3)
                if k == 1 and j > 0 and j % 2 == 1 and present(it, j + 3):
                    load_ctx(it, j // 2 + 2)
                if k == 2 and present(it, j - 3):
                    wait_for(sp, fin_added, it * CHUNKS + NCH * (j - 2))
                    t = it * UNROLL + j - 3
                    sp.dma_start(out[rows(t), :], x1[(j - 3) % 4][:]).then_inc(stored[(j - 3) % 4], 16)

            iterate(sp, slot)
            for j in range(4):
                sp.wait_ge(stored[j], 16 * ITERS)

        @block.tensor
        def _(pe):
            def scores(it, j, k):
                g, batch = k // 2, j // 2 % 2
                if k % 4 == 0:
                    wait_for(pe, qt_moved, it * CHUNKS + NCH * j + k // 4 + 1)
                if j % 2 == 0 and k % 8 == 0:
                    wait_for(pe, kt_moved, (it * BATCHES + j // 2) * 4 + 2 + k // 4)
                wait_for(pe, masked, 2 * (it * PAIRS + SLOTS * j + k - 1))
                for r in range(2):
                    to = s_bank[k % 2][:, r * SEQ:(r + 1) * SEQ]
                    q = qT[j % 2][:, 2 * k + r, :]
                    pe.matmul(to, q, kT[batch][0][:, g, :], start=True, stop=False)
                    last = pe.matmul(to, q, kT[batch][1][:, g, :], start=False, stop=True)
                last.then_inc(scores_ready, 1)

            def turn(it, n):
                wait_for(pe, shifted, it * PAIRS + n + 1)
                wait_for(pe, probs_ready, it * PAIRS + n - 1)
                for c in range(TPB):
                    for r in range(2):
                        last = pe.transpose(t_bank[n % 2][:, (2 * c + r) * P:(2 * c + r + 1) * P],
                                            scores_sb[n % 4][:, r, c * P:(c + 1) * P], ident32[:])
                last.then_inc(turned, 1)

            def values(it, j, k, n):
                g, batch = k // 2, j // 2 % 2
                wait_for(pe, rest_ready, it * PAIRS + n + 1)
                if j % 2 == 0 and k == 0:
                    wait_for(pe, v_ready, (it * BATCHES + j // 2 + 1) * 2)
                if k % 2 == 0:
                    wait_for(pe, normed, it * GROUPS + NG * j + g - 1)
                for r in range(2):
                    at = (2 * (k % 2) + r) * (HD + 1)
                    to = o_bank[g % 2][:, at:at + HD + 1]
                    for c in range(TPB):
                        high = probs[n % RING][:, c, r, :].bitcast(BF16)[:, 1::2]
                        low = probs_low[n % RING][:, c, r, :]
                        v1 = v_high[batch][:, c, g, 0:HD + 1]
                        pe.matmul(to, high, v1, start=c == 0, stop=False)
                        pe.matmul(to[:, 0:HD], high, v_low[batch][:, c, g, :], start=False, stop=False)
                        last = pe.matmul(to, low, v1, start=False, stop=c == TPB - 1)
                last.then_inc(pv_done, 1)

            def emptied(it, j, task, part):
                if task == "QT":
                    pe.wait_ge(qt_moved, it * CHUNKS + NCH * j + part + 1)
                elif task == "KT":
                    pe.wait_ge(kt_moved, (it * BATCHES + j // 2) * 4 + part + 1)
                elif task == "XT":
                    pe.wait_ge(xt_low, it * CHUNKS + NCH * j + part + 1)
                elif task == "LT":
                    pe.wait_ge(lt_moved, it * UNROLL + j + 1)
                elif task == "LOW":
                    pe.wait_ge(low_moved, it * UNROLL + j + 1)
                else:
                    pe.wait_ge(fin_added, it * CHUNKS + NCH * j + part + 1)

            def q_turn(b, it, j, part):
                pe.wait_ge(ql_done, it * CHUNKS + NCH * j + part + 1)
                for h in range(8):
                    last = pe.transpose(b.bitcast(F16)[:, h * P:(h + 1) * P],
                                        q_split[:, 8 * part + h, :, :].rearrange("p a d -> p (a d)"), ident16[:])
                last.then_inc(qt_turned, 1)

            def k_turn(b, it, batch, part):
                pe.wait_ge(k_step, (it * BATCHES + batch) * K_STEPS + (15 if part % 2 else 13))
                for g in range(4):
                    for c in range(TPB):
                        src = k_twice[:, part % 2, c, 4 * (part // 2) + g, :, :].rearrange("p a d -> p (a d)")
                        last = pe.transpose(b.bitcast(F16)[:, (2 * g + c) * P:(2 * g + c + 1) * P], src, ident16[:])
                last.then_inc(kt_turned, 1)

            def side(it, j, task, part, b):
                if task == "QT":
                    q_turn(b, it, j, part)
                elif task == "KT":
                    k_turn(b, it, j // 2, part)
                elif task == "XT":
                    pe.wait_ge(normalised[1], 2 * (it * UNROLL + j) + part // 2 + 1)
                    for c in range(4):
                        at = (4 * part + c) * P
                        last = pe.transpose(b[:, c * P:(c + 1) * P], xn2[:, at:at + P], ident32[:])
                    last.then_inc(xt_turned, 1)
                elif task == "LOW":
                    if part == 0:
                        pe.wait_ge(xt_low, it * CHUNKS + NCH * (j + 1))
                        if isinstance(it, int) and it == 0:
                            pe.wait_ge(w_step, W_DOWN)
                    to = b[:, 0:ROUTED]
                    for c in range(part * DCH // 2, (part + 1) * DCH // 2):
                        high, low = x2T[:, c // 4, 0, c % 4, :], x2T[:, c // 4, 1, c % 4, :]
                        pe.matmul(to, high, w_high[:, c, :], start=c == 0, stop=False)
                        pe.matmul(to, high, w_low[:, c, :], start=False, stop=False)
                        last = pe.matmul(to, low, w_high[:, c, :], start=False, stop=c == DCH - 1)
                    if part == 1:
                        last.then_inc(low_ready, 1)
                elif task == "LT":
                    pe.wait_ge(router_step, (it * UNROLL + j + 1) * ROUTER_STEPS)
                    for s in range(2):
                        last = pe.transpose(b.bitcast(F16)[:, s * P:(s + 1) * P], routed_split[:, s, :], ident16[:])
                    last.then_inc(lt_turned, 1)
                else:
                    if part == 0:
                        pe.wait_ge(lt_moved, it * UNROLL + j + 1)
                        if isinstance(it, int) and it == 0:
                            pe.wait_ge(w_step, W_ALL)
                    cols = slice(part * CH, (part + 1) * CH)
                    pe.matmul(b[:], routedT[:, 0, :], b_high[:, cols], start=True, stop=False)
                    pe.matmul(b[:], routedT[:, 0, :], b_low[:, cols], start=False, stop=False)
                    pe.matmul(b[:], routedT[:, 1, :], b_high[:, cols], start=False, stop=True).then_inc(fin_ready, 1)

            def bank_holder(it, j, m):
                for back in range(m - 1, m - len(side_tasks), -1):
                    js, d, task, part, b = side_tasks[back % len(side_tasks)]
                    at = js + j - j % UNROLL - (UNROLL if back < 0 else 0) + d
                    if b == side_tasks[m][4] and present(it, at):
                        emptied(it, at, task, part)
                        return

            def slot(it, j, k):
                jt, _, nt = pair(j, k, LAG_T)
                jv, kv, nv = pair(j, k, LAG_PV)
                for entry in PE_SLOTS[k]:
                    if entry == "SCORES":
                        if present(it, j):
                            scores(it, j, k)
                    elif entry == "TURN":
                        if present(it, jt):
                            turn(it, nt)
                    elif entry == "VALUES":
                        if present(it, jv):
                            values(it, jv, kv, nv)
                    elif side_tile(it, j, entry) is not None:
                        m = next(m for m, t in enumerate(side_tasks) if t[:4] == (j % UNROLL, *entry))
                        if entry[1:] != ("LOW", 1):
                            bank_holder(it, j, m)
                        side(it, side_tile(it, j, entry), entry[1], entry[2], m_bank[side_tasks[m][4]])

            pe.wait_ge(idents_ready, 2)
            iterate(pe, slot)

        @block.vector
        def _(dve):
            def mask_and_max(it, j, k, r):
                n = SLOTS * j + k
                if r == 0:
                    wait_for(dve, scores_ready, it * PAIRS + n + 1)
                    wait_for(dve, turned, it * PAIRS + n - 3)
                    if k == 0 and j % 2 == 0:
                        wait_for(dve, k_step, (it * BATCHES + j // 2) * K_STEPS + 9)
                    dve.sem_inc(gate, 1)
                dve.tensor_tensor_reduce(
                    scores_sb[n % 4][:, r, :], s_bank[n % 2][:, r * SEQ:(r + 1) * SEQ],
                    mask_scaled[j // 2 % 2][:, j % 2, :], -1.0, BIG, ALU.add, ALU.min,
                    neg_max[:, n % 4, r:r + 1]).then_inc(masked, 1)

            def sums_reciprocal(it, j, g):
                dve.wait_ge(pv_done, it * PAIRS + SLOTS * j + 2 * g + 2)
                o = o_bank[g % 2][:, 0:REP * (HD + 1)].rearrange("p (h d) -> p h d", h=REP)
                dve.reciprocal(recip[:, g % 2, :].unsqueeze(2), o[:, :, HD:HD + 1]).then_inc(recip_ready, 1)

            def norm(it, j, g):
                if g == 0:
                    wait_for(dve, stored[j % 4], 16 * (it + j // 4))
                o = o_bank[g % 2][:, 0:REP * (HD + 1)].rearrange("p (h d) -> p h d", h=REP)
                dve.wait_ge(recip_ready, it * GROUPS + NG * j + g + 1)
                to = x1[j % 4][:, g * REP * HD:(g + 1) * REP * HD].rearrange("p (h d) -> p h d", h=REP)
                dve.scalar_tensor_tensor(to, o[:, :, 0:HD], v_unscale[:, j // 2 % 2:j // 2 % 2 + 1],
                                         recip[:, g % 2, :].unsqueeze(2).to_broadcast([P, REP, HD]),
                                         ALU.mult, ALU.mult).then_inc(normed, 1)

            def x2_low(it, j, c):
                dve.wait_ge(xt_high, it * CHUNKS + NCH * j + c + 1)
                b = side_bank(j, "XT", c)
                dve.tensor_tensor(x2T[:, c, 1, :, :].rearrange("p c s -> p (c s)"), b[:],
                                  x2T[:, c, 0, :, :].rearrange("p c s -> p (c s)"), ALU.subtract).then_inc(xt_low, 1)

            def stats(it, j, c, which):
                src = (x_in, x1)[which][j % 4]
                if which:
                    dve.wait_ge(added, it * CHUNKS + NCH * j + c + 1)
                elif c == 0:
                    dve.wait_ge(x_loaded[j % 4], 16 * (it + 1 + j // 4))
                if c == 0:
                    wait_for(dve, ln_step, (it * UNROLL + j + (-1, 2)[which]) * LN_STEPS + 2)
                dve.bn_stats(ln_stats[which][:, 6 * c:6 * c + 6], src[:, c * CH:(c + 1) * CH]).then_inc(stats_done[which], 1)

            def ln_op(it, j, m):
                base = (it * UNROLL + j + 2) * LN_STEPS
                mean, var = (ln_mv[:, :, i:i + 1] for i in range(2))
                ve, y, w, nb = (ln_work[:, i, :].unsqueeze(2) for i in range(4))
                wait_for(dve, ln_step, base + m)
                if m < 2:
                    at = j + (2, -1)[m]
                    if present(it, at):
                        dve.wait_ge(stats_done[m], it * CHUNKS + NCH * at + NCH)
                        dve.sem_inc(gate, 1)
                        op = dve.bn_aggr(ln_mv[:, m, :], ln_stats[m][:])
                    else:
                        op = dve.memset(ln_mv[:, m, :], 1.0)
                elif m == 2:
                    op = dve.tensor_scalar(ve, var, EPS, None, ALU.add)
                elif m == 3:
                    op = dve.tensor_scalar(w.bitcast(I32), ve.bitcast(I32), 1, None, ALU.logical_shift_right)
                elif m == 4:
                    for which, at in enumerate((j + 1, j - 2)):
                        if present(it, at):
                            dve.wait_ge(normalised[which], 2 * (it * UNROLL + at + 1))
                    op = dve.tensor_scalar(y.bitcast(I32), w.bitcast(I32), -1.0, float(RSQRT_SEED), ALU.mult, ALU.add)
                elif m == 14:
                    op = dve.scalar_tensor_tensor(nb, mean, -1.0, y, ALU.mult, ALU.mult)
                elif m % 3 == 2:
                    op = dve.scalar_tensor_tensor(w, y, 1.0, y, ALU.mult, ALU.mult)
                elif m % 3 == 0:
                    op = dve.scalar_tensor_tensor(w, w, -0.5 * (Q_SCALE if m == 12 else 1.0), ve, ALU.mult, ALU.mult)
                else:
                    op = dve.scalar_tensor_tensor(y, w, 1.5 * (Q_SCALE if m == 13 else 1.0), y, ALU.add, ALU.mult)
                op.then_inc(ln_step, 1)

            def normalise(it, j, half):
                cols = slice(half * DM // 2, (half + 1) * DM // 2)
                dve.wait_ge(ln_step, (it * UNROLL + j + 4) * LN_STEPS)
                wait_for(dve, xt_turned, it * CHUNKS + NCH * j)
                dve.tensor_scalar(xn2[:, cols], x1[j % 4][:, cols], ln_work[:, 1, 1:2],
                                  ln_work[:, 3, 1:2], ALU.mult, ALU.add).then_inc(normalised[1], 1)

            def router_op(it, j, m):
                base = (it * UNROLL + j) * ROUTER_STEPS
                if m == 0:
                    dve.wait_ge(low_moved, it * UNROLL + j + 1)
                    op = dve.scalar_tensor_tensor(logits[:], low_sb[:, LOWS:ROUTED], w_pow[:, 9:10], br_sb[:],
                                                  ALU.mult, ALU.add)
                elif m == 2:
                    dve.wait_ge(router_exp, it * UNROLL + j + 1)
                    op = dve.reciprocal(gate_rec[:], gate_sum[:])
                else:
                    dve.wait_ge(router_step, base + m)
                if m == 1:
                    op = dve.tensor_reduce(gate_max[:], logits[:], AX.X, ALU.max, negate=True)
                elif m == 3:
                    op = dve.scalar_tensor_tensor(routed[:].rearrange("p (e r) -> p e r", e=EXPERTS),
                                                  low_sb[:, 0:LOWS].rearrange("p (e r) -> p e r", e=EXPERTS),
                                                  gate_rec[:], gates[:].unsqueeze(2).to_broadcast([P, EXPERTS, RANK]),
                                                  ALU.mult, ALU.mult)
                elif m == 4:
                    wait_for(dve, lt_turned, it * UNROLL + j)
                    op = dve.tensor_copy(routed_split[:, 0, :], routed[:])
                elif m == 5:
                    op = dve.tensor_tensor(routed_split[:, 1, :], routed[:], routed_split[:, 0, :], ALU.subtract)
                op.then_inc(router_step, 1)

            def finish(it, j, c):
                b = side_bank(j, "FIN", c)
                dve.wait_ge(fin_ready, it * CHUNKS + NCH * j + c + 1)
                cols = slice(c * CH, (c + 1) * CH)
                dve.scalar_tensor_tensor(x1[j % 4][:, cols], b[:], w_pow[:, 10:11], x1[j % 4][:, cols],
                                         ALU.mult, ALU.add).then_inc(fin_added, 1)

            def ctx_maximum(it, b):
                dve.wait_ge(ctx_loaded, (it * BATCHES + b + 1) * 16)
                dve.tensor_reduce(ctx_max[:], ctx_in[:], AX.XY, ALU.max, apply_absolute_value=True).then_inc(k_step, 1)

            def ctx_op(it, b, m):
                base = (it * BATCHES + b) * K_STEPS
                power, inv, k_scale, m_scale, top = (ctx_pow[:, i:i + 1] for i in range(5))
                before = it * BATCHES + b - 1
                if m == 0:
                    dve.wait_ge(ctx_max_ready, it * BATCHES + b + 1)
                    op = dve.tensor_scalar(top, ctx_max_all[:], LEAST, None, ALU.max)
                else:
                    dve.wait_ge(k_step, base + (7 if m > 6 else min(m + 1, 4)) + (m > 6))
                if m == 1:
                    op = dve.tensor_scalar(power.bitcast(U32), top.bitcast(U32), EXPONENT, None, ALU.bitwise_and)
                elif m == 2:
                    op = dve.reciprocal(inv, power)
                elif m == 3:
                    op = dve.tensor_scalar(k_scale, inv, 4096.0, None, ALU.mult)
                elif m == 4:
                    wait_for(dve, probs_ready, before * TPB * SLOTS)
                    op = dve.tensor_scalar(exp_scale[:, b % 2:b % 2 + 1], power, 2.0 ** -23, None, ALU.mult)
                elif m == 5:
                    wait_for(dve, normed, before * TPB * NG)
                    op = dve.tensor_scalar(v_unscale[:, b % 2:b % 2 + 1], power, 2.0 ** -12, None, ALU.mult)
                elif m == 6:
                    op = dve.tensor_scalar(m_scale, inv, 2.0 ** 23, None, ALU.mult)
                elif m == 7:
                    wait_for(dve, masked, before * TPB * NH)
                    if isinstance(it, int) and it == 0:
                        dve.wait_ge(mask_loaded, 16)
                    op = dve.tensor_scalar(mask_scaled[b % 2][:], mask_in[:], m_scale, None, ALU.mult)
                op.then_inc(k_step, 1)

            def values_scaled(it, b, m):
                k_scale = ctx_pow[:, 2:3]
                if m == 0:
                    wait_for(dve, pv_done, (it * BATCHES + b - 1) * TPB * SLOTS)
                    src = ctx_in[:].rearrange("p c (g d) -> p (c g) d", g=NG)
                    dve.tensor_scalar(v_high[b % 2][:].rearrange("p c g d -> p (c g) d")[:, :, 0:HD], src, k_scale,
                                      None, ALU.mult).then_inc(k_step, 1)
                else:
                    dve.wait_ge(k_step, (it * BATCHES + b) * K_STEPS + 10)
                    dve.tensor_scalar(ctx_in[:], ctx_in[:], k_scale, None, ALU.mult).then_inc(k_step, 1)

            def keys_twice(it, b, part):
                base = (it * BATCHES + b) * K_STEPS
                if part == 0:
                    dve.wait_ge(k_step, base + 10)
                    wait_for(dve, kt_turned, (it * BATCHES + b) * 4)
                else:
                    dve.wait_ge(v_ready, (it * BATCHES + b + 1) * 2)
                src = (v_high, v_low)[part][b % 2]
                for c in range(TPB):
                    dve.tensor_copy(k_twice[:, part, c, :, :, :],
                                    src[:, c, :, 0:HD].unsqueeze(2).to_broadcast([P, NG, 2, HD])).then_inc(k_step, 1)

            def weights(m):
                a_in, r_in, b_in = x1[3][:], x1[1][:, 0:DCH * EXPERTS], x1[2][:]
                wh, wl = w_high[:], w_low[:]
                three = lambda ap, n: ap.rearrange("p (c n) -> p c n", c=DCH)
                if m == 0:
                    dve.wait_ge(weights_loaded, 64)
                    for i, w in enumerate((a_in, r_in, b_in)):
                        dve.tensor_reduce(w_max[:, i:i + 1], w, AX.X, ALU.max, apply_absolute_value=True).then_inc(w_step, 1)
                elif m == 1:
                    p = lambda a, b: w_pow[:, a:b]
                    dve.wait_ge(w_max_ready, 1)
                    dve.tensor_scalar(p(0, 3), w_max_all[:], LEAST, None, ALU.max).then_inc(w_step, 1)
                    dve.wait_ge(w_step, 4)
                    dve.tensor_scalar(p(3, 6).bitcast(U32), p(0, 3).bitcast(U32), EXPONENT, None, ALU.bitwise_and).then_inc(w_step, 1)
                    dve.wait_ge(w_step, 5)
                    dve.reciprocal(p(11, 14), p(3, 6)).then_inc(w_step, 1)
                    dve.wait_ge(w_step, 6)
                    dve.tensor_scalar(p(6, 9), p(11, 14), 4096.0, None, ALU.mult).then_inc(w_step, 1)
                    dve.tensor_scalar(p(9, 10), p(4, 5), 2.0 ** -3, None, ALU.mult).then_inc(w_step, 1)
                    dve.tensor_scalar(p(10, 11), p(3, 4), p(5, 6), 2.0 ** -11, ALU.mult, ALU.mult).then_inc(w_step, 1)
                    dve.wait_ge(w_step, 9)
                elif m == 2:
                    dve.tensor_scalar(wh[:, :, 0:LOWS], three(a_in, LOWS), w_pow[:, 6:7], None, ALU.mult).then_inc(w_step, 1)
                    dve.wait_ge(w_step, 10)
                    dve.tensor_scalar(a_in, a_in, w_pow[:, 6:7], None, ALU.mult).then_inc(w_step, 1)
                elif m == 3:
                    dve.wait_ge(w_step, 11)
                    dve.tensor_tensor(wl[:, :, 0:LOWS], three(a_in, LOWS), wh[:, :, 0:LOWS], ALU.subtract).then_inc(w_step, 1)
                elif m == 4:
                    dve.tensor_scalar(wh[:, :, LOWS:ROUTED], three(r_in, EXPERTS), w_pow[:, 7:8], None, ALU.mult).then_inc(w_step, 1)
                    dve.wait_ge(w_step, 13)
                    dve.tensor_scalar(r_in, r_in, w_pow[:, 7:8], None, ALU.mult).then_inc(w_step, 1)
                    dve.wait_ge(w_step, 14)
                    dve.tensor_tensor(wl[:, :, LOWS:ROUTED], three(r_in, EXPERTS), wh[:, :, LOWS:ROUTED], ALU.subtract).then_inc(w_step, 1)
                elif m == 5:
                    dve.tensor_scalar(b_high[:], b_in, w_pow[:, 8:9], None, ALU.mult).then_inc(w_step, 1)
                    dve.wait_ge(w_step, 16)
                    dve.tensor_scalar(b_in, b_in, w_pow[:, 8:9], None, ALU.mult).then_inc(w_step, 1)
                elif m == 6:
                    dve.wait_ge(w_step, 17)
                    dve.tensor_tensor(b_low[:], b_in, b_high[:], ALU.subtract).then_inc(w_step, 1)

            def side(it, j, task, part):
                if task == "REC":
                    sums_reciprocal(it, j, part)
                elif task == "NORM":
                    norm(it, j, part)
                elif task == "XTL":
                    x2_low(it, j, part)
                elif task == "BN1":
                    stats(it, j, part, 0)
                elif task == "BN2":
                    stats(it, j, part, 1)
                elif task == "XN2":
                    normalise(it, j, part)
                elif task == "R":
                    router_op(it, j, part)
                elif task == "FIN":
                    finish(it, j, part)
                elif task == "KMAX":
                    ctx_maximum(it, j // 2)
                elif task == "KOP":
                    ctx_op(it, j // 2, part)
                elif task == "KV":
                    values_scaled(it, j // 2, part)
                else:
                    keys_twice(it, j // 2, part)

            def slot(it, j, k):
                for entry in DVE_SLOTS[k]:
                    if entry in ("MASK0", "MASK1"):
                        if present(it, j):
                            mask_and_max(it, j, k, int(entry == "MASK1"))
                    elif entry[1] == "LN":
                        if present(it, j + 2) or present(it, j - 1):
                            ln_op(it, j, entry[2])
                    elif side_tile(it, j, entry) is not None:
                        side(it, side_tile(it, j, entry), entry[1], entry[2])
                if isinstance(it, int) and it == 0 and j == 0 and 5 <= k < 12:
                    weights(k - 5)

            for b in range(2):
                dve.memset(v_high[b][:, :, :, HD:HD + 2], 1.0).then_inc(ones_ready, 1)
            iterate(dve, slot)

        @block.scalar
        def _(act):
            def exponentiate(it, j, n):
                wait_for(act, turned, it * PAIRS + n + 1)
                wait_for(act, pv_done, it * PAIRS + n - RING + 1)
                act.activation(probs[n % RING][:].rearrange("p c r s -> p (c r s)"), t_bank[n % 2][:], ACT.Exp,
                               scale=exp_scale[:, j // 2 % 2:j // 2 % 2 + 1]).then_inc(probs_ready, 1)

            def shift(it, n):
                for r in range(2):
                    wait_for(act, masked, 2 * (it * PAIRS + n) + r + 1)
                    s = scores_sb[n % 4][:, r, :]
                    last = act.activation(s, s, ACT.Identity, bias=neg_max[:, n % 4, r:r + 1], scale=-1.0)
                last.then_inc(shifted, 1)

            def words(ap):
                return ap.bitcast(F32)

            def q_move(b, it, j, part):
                act.wait_ge(qt_turned, it * CHUNKS + NCH * j + part + 1)
                wait_for(act, scores_ready, it * PAIRS + SLOTS * (j - 1))
                act.copy(words(qT[j % 2][:, 8 * part:8 * part + 8, :].rearrange("p h s -> p (h s)")),
                         b[:]).then_inc(qt_moved, 1)

            def k_move(b, it, batch, part):
                act.wait_ge(kt_turned, (it * BATCHES + batch) * 4 + part + 1)
                wait_for(act, scores_ready, (it * BATCHES + batch - 1) * TPB * SLOTS)
                half = 4 * (part // 2)
                act.copy(words(kT[batch % 2][part % 2][:, half:half + 4, :].rearrange("p g t -> p (g t)")),
                         b[:]).then_inc(kt_moved, 1)

            def q_high(it, j, half):
                act.wait_ge(normalised[0], 2 * (it * UNROLL + j) + half + 1)
                wait_for(act, qt_turned, it * CHUNKS + NCH * j)
                hs = slice(half * NH // 2, (half + 1) * NH // 2)
                act.copy(q_split[:, hs, 0, :], xn1[:].rearrange("p (h d) -> p h d", h=NH)[:, hs, :]).then_inc(qh_done, 1)

            def normalise(it, j, half):
                cols = slice(half * DM // 2, (half + 1) * DM // 2)
                act.wait_ge(ln_step, (it * UNROLL + j + 1) * LN_STEPS)
                wait_for(act, ql_done, it * CHUNKS + NCH * j)
                act.activation(xn1[:, cols], x_in[j % 4][:, cols], ACT.Identity, bias=ln_work[:, 3, 0:1],
                               scale=ln_work[:, 1, 0:1]).then_inc(normalised[0], 1)

            def router_exp_sum(it, j):
                act.wait_ge(router_step, (it * UNROLL + j) * ROUTER_STEPS + 2)
                act.activation(gates[:], logits[:], ACT.Exp, bias=gate_max[:], accum_out=gate_sum[:]).then_inc(router_exp, 1)

            def side(it, j, task, part):
                if task in ("QT", "KT", "XT", "LOW", "LT"):
                    b = side_bank(j, task, part)
                if task == "QH":
                    q_high(it, j, part)
                elif task == "XN1":
                    normalise(it, j, part)
                elif task == "REXP":
                    router_exp_sum(it, j)
                elif task == "QT":
                    q_move(b, it, j, part)
                elif task == "KT":
                    k_move(b, it, j // 2, part)
                elif task == "XT":
                    act.wait_ge(xt_turned, it * CHUNKS + NCH * j + part + 1)
                    wait_for(act, low_ready, it * UNROLL + j)
                    act.copy(x2T[:, part, 0, :, :].rearrange("p c s -> p (c s)"), b[:]).then_inc(xt_high, 1)
                elif task == "LOW" and part == 1:
                    act.wait_ge(low_ready, it * UNROLL + j + 1)
                    wait_for(act, router_step, (it * UNROLL + j) * ROUTER_STEPS)
                    act.mul(low_sb[:], b[:, 0:ROUTED], 2.0 ** -17).then_inc(low_moved, 1)
                elif task == "LT":
                    act.wait_ge(lt_turned, it * UNROLL + j + 1)
                    wait_for(act, fin_ready, it * CHUNKS + NCH * j)
                    act.copy(words(routedT[:].rearrange("p a s -> p (a s)")), b[:, 0:P]).then_inc(lt_moved, 1)

            def slot(it, j, k):
                je, _, ne = pair(j, k, LAG_EXP)
                js, _, ns = pair(j, k, LAG_SHIFT)
                for entry in ACT_SLOTS[k]:
                    if entry == "EXP":
                        if present(it, je):
                            exponentiate(it, je, ne)
                    elif entry == "SHIFT":
                        if present(it, js):
                            shift(it, ns)
                    elif side_tile(it, j, entry) is not None:
                        side(it, side_tile(it, j, entry), entry[1], entry[2])

            iterate(act, slot)

        @block.gpsimd
        def _(pool):
            def rest(it, n):
                wait_for(pool, probs_ready, it * PAIRS + n + 1)
                p = probs[n % RING][:].rearrange("p c r s -> p (c r s)")
                pool.tensor_tensor(probs_low[n % RING][:].rearrange("p c r s -> p (c r s)"), p, p.bitcast(BF16)[:, 1::2],
                                   ALU.subtract).then_inc(rest_ready, 1)

            def q_low(it, j, c):
                pool.wait_ge(qh_done, (it * UNROLL + j) * 2 + c // 2 + 1)
                hs = slice(8 * c, 8 * c + 8)
                pool.tensor_tensor(q_split[:, hs, 1, :], xn1[:].rearrange("p (h d) -> p h d", h=NH)[:, hs, :],
                                   q_split[:, hs, 0, :], ALU.subtract).then_inc(ql_done, 1)

            def residual(it, j, c):
                pool.wait_ge(normed, it * GROUPS + NG * j + 2 * c + 2)
                cols = slice(c * CH, (c + 1) * CH)
                pool.tensor_tensor(x1[j % 4][:, cols], x1[j % 4][:, cols], x_in[j % 4][:, cols],
                                   ALU.add).then_inc(added, 1)

            def ctx_all(it, b):
                pool.wait_ge(k_step, (it * BATCHES + b) * K_STEPS + 1)
                pool.sem_inc(pool_gate, 1)
                pool.partition_all_reduce(ctx_max_all[:], ctx_max[:], P, bass.bass_isa.ReduceOp.max).then_inc(ctx_max_ready, 1)

            def values_low(it, b, c):
                pool.wait_ge(k_step, (it * BATCHES + b) * K_STEPS + 11)
                pool.tensor_tensor(v_low[b % 2][:, c, :, :], ctx_in[:, c, :].rearrange("p (g d) -> p g d", g=NG),
                                   v_high[b % 2][:, c, :, 0:HD], ALU.subtract).then_inc(v_ready, 1)

            def slot(it, j, k):
                jr, _, n = pair(j, k, LAG_REST)
                for entry in POOL_SLOTS[k]:
                    if entry == "REST":
                        if present(it, jr):
                            rest(it, n)
                    elif side_tile(it, j, entry) is not None:
                        at, task, part = side_tile(it, j, entry), entry[1], entry[2]
                        if task == "QL":
                            q_low(it, at, part)
                        elif task == "RES":
                            residual(it, at, part)
                        elif task == "KALL":
                            ctx_all(it, at // 2)
                        else:
                            values_low(it, at // 2, part)
                if isinstance(it, int) and it == 0 and j == 0 and k == 5:
                    pool.wait_ge(w_step, 3)
                    pool.partition_all_reduce(w_max_all[:], w_max[:], P, bass.bass_isa.ReduceOp.max).then_inc(w_max_ready, 1)

            ones_at = sem("ones_at")
            for i, ident in enumerate((ident32, ident16)):
                pool.memset(ident[:], 0.0).then_inc(ones_at, 1)
                pool.wait_ge(ones_at, i + 1)
                pool.affine_select(out=ident[:], in_=ident[:], compare_op=ALU.not_equal, fill=1.0, base=0,
                                   pattern=[[-1, P]], channel_multiplier=1).then_inc(idents_ready, 1)
            iterate(pool, slot)


def kernel(x, ctx_1024, mask_SxS2_ff0, L0_ffn_A, L0_ffn_B, L0_ffn_Wr, L0_ffn_br):
    import numpy as np
    import concourse.bacc as bacc
    from concourse.bass_utils import run_bass_kernel_spmd

    h, r, d = L0_ffn_A.shape
    arrays = {
        "x": np.asarray(x).reshape(-1, d),
        "ctx": np.asarray(ctx_1024).reshape(-1, ctx_1024.shape[-1]),
        "mask": np.asarray(mask_SxS2_ff0),
        "wa": np.asarray(L0_ffn_A).reshape(h * r, d).T,
        "wr": np.asarray(L0_ffn_Wr).T,
        "wb": np.asarray(L0_ffn_B).transpose(0, 2, 1).reshape(h * r, d),
        "br": np.broadcast_to(np.asarray(L0_ffn_br), (P, h)),
    }
    arrays = {f"in_{k}": np.ascontiguousarray(a) for k, a in arrays.items()}
    nc = bacc.Bacc("TRN2", target_bir_lowering=False, num_devices=1)
    args = [nc.dram_tensor(k, a.shape, mybir.dt.from_np(a.dtype), kind="ExternalInput").ap() for k, a in arrays.items()]
    out = nc.dram_tensor("out", arrays["in_x"].shape, F32, kind="ExternalOutput").ap()
    build(nc, *args, out)
    got = run_bass_kernel_spmd(nc, [arrays], core_ids=[0]).results[0]["out"]
    return got.reshape(x.shape)
```
